# Optimizing a Trainium2 kernel written in Bass

```python
import numpy as np
import jax
import jax.numpy as jnp

def _softmax(x, axis=-1):
    return jax.nn.softmax(x, axis=axis)

def _gelu(x):
    return jax.nn.gelu(x, approximate=True)

def _silu(x):
    return jax.nn.silu(x)

def _sigmoid(x):
    return jax.nn.sigmoid(x)

def _layernorm(x, axis=-1, eps=1e-05):
    m = jnp.mean(x, axis=axis, keepdims=True)
    v = jnp.var(x, axis=axis, keepdims=True)
    return (x - m) / jnp.sqrt(v + eps)

def _scatter_add(tgt, idx, src, axis=0):
    return tgt.at[idx].add(src)

def _segment_sum(src, seg, n):
    return jax.ops.segment_sum(src, seg, n)
kernel_name = 'mk_gnn_resnorm_d2_gnn_r8_e5390e'

def setup_inputs(seed: int=0):
    np.random.seed(seed)
    _w = jnp.asarray

    def _rec_inputs():
        import jax
        import jax.numpy as jnp
        _gk = jax.random.key(seed)
        x = -0.000202 + 1 * jax.random.normal(jax.random.fold_in(_gk, 1), (6250, 128), jnp.float32)
        _s = jax.random.randint(jax.random.fold_in(_gk, 2), (100000,), 0, 6250, jnp.int32)
        _d = jax.random.randint(jax.random.fold_in(_gk, 3), (100000,), 0, 6250, jnp.int32)
        _loop = jnp.arange(6250, dtype=jnp.int32)
        src = jnp.concatenate([_s, _d, _loop])
        dst = jnp.concatenate([_d, _s, _loop])
        _o = jnp.argsort(dst, stable=True)
        src = src[_o]
        dst = dst[_o]
        edge_weight = jax.random.uniform(jax.random.fold_in(_gk, 13), (206250,), jnp.float32, 0.0, 1)
        return (x, src, dst, edge_weight)
    x, src, dst, edge_weight = _rec_inputs()

    def _L0_gnn_setup():
        import jax, jax.numpy as jnp
        import numpy as np
        N_NODES = 6250
        N_EDGES = 200000
        IN_CH = 128
        HEAD = 8
        OUT_CH = 16
        LEAKY_ALPHA = 0.3
        key = jax.random.key(seed)
        k1, k2, k3, k4, k5, k6 = jax.random.split(key, 6)
        x = jax.random.normal(k1, (N_NODES, IN_CH), dtype=jnp.float32)
        w1 = jax.random.normal(k2, (IN_CH, HEAD * OUT_CH), dtype=jnp.float32) * (1.0 / np.sqrt(IN_CH))
        w2 = jax.random.normal(k3, (IN_CH, HEAD * OUT_CH), dtype=jnp.float32) * (1.0 / np.sqrt(IN_CH))
        a = jax.random.normal(k4, (1, HEAD * OUT_CH), dtype=jnp.float32) * 0.1
        src = jax.random.randint(k5, (N_EDGES,), 0, N_NODES, dtype=jnp.int32)
        tgt = jax.random.randint(k6, (N_EDGES,), 0, N_NODES, dtype=jnp.int32)
        return {'x': x, 'w1': w1, 'w2': w2, 'a': a, 'src': src, 'tgt': tgt}
    _L0_gnn_all = _L0_gnn_setup()
    _L0_gnn_in = {k: v for k, v in _L0_gnn_all.items() if k in ('w1', 'w2', 'a')}
    del _L0_gnn_all

    def _L1_gnn_setup():
        import jax, jax.numpy as jnp
        import numpy as np
        N_NODES = 1250
        N_EDGES = 80000
        FEAT_DIM = 128
        AGG_STRENGTH = 0.3
        EPS = 1e-08
        key = jax.random.key(seed)
        k1, k2, k3, k4 = jax.random.split(key, 4)
        features = jax.random.normal(k1, (N_NODES, FEAT_DIM), dtype=jnp.float32)
        edge_weights = jax.random.uniform(k2, (N_EDGES,), dtype=jnp.float32)
        src = jax.random.randint(k3, (N_EDGES,), 0, N_NODES, dtype=jnp.int32)
        tgt = jax.random.randint(k4, (N_EDGES,), 0, N_NODES, dtype=jnp.int32)
        edges = jnp.stack([src, tgt], axis=1)
        return {'features': features, 'edge_weights': edge_weights, 'edges': edges}
    _L1_gnn_all = _L1_gnn_setup()
    _L1_gnn_in = {k: v for k, v in _L1_gnn_all.items() if k in ()}
    del _L1_gnn_all
    return {'x': x, 'src': src, 'dst': dst, 'edge_weight': edge_weight, 'L0_gnn_w1': _L0_gnn_in['w1'], 'L0_gnn_w2': _L0_gnn_in['w2'], 'L0_gnn_a': _L0_gnn_in['a']}

def reference(x, src, dst, edge_weight, L0_gnn_w1, L0_gnn_w2, L0_gnn_a):
    import jax
    import jax.numpy as jnp

    def _L0_gnn_ref(x, w1, w2, a, src, tgt):
        import jax, jax.numpy as jnp
        import numpy as np
        N_NODES = 6250
        N_EDGES = 200000
        IN_CH = 128
        HEAD = 8
        OUT_CH = 16
        LEAKY_ALPHA = 0.3
        hi = x[src] @ w1
        hj = x[tgt] @ w2
        e = jax.nn.leaky_relu(hi + hj, negative_slope=LEAKY_ALPHA)
        e = e * a
        logits = e.reshape(-1, HEAD, OUT_CH).sum(axis=-1)
        seg_max = jax.ops.segment_max(logits, tgt, num_segments=N_NODES)
        seg_max = jnp.where(jnp.isfinite(seg_max), seg_max, 0.0)
        exp = jnp.exp(logits - seg_max[tgt])
        seg_sum = jax.ops.segment_sum(exp, tgt, num_segments=N_NODES)
        attn = exp / seg_sum[tgt]
        msg = hi.reshape(-1, HEAD, OUT_CH) * attn[:, :, None]
        out = jax.ops.segment_sum(msg, tgt, num_segments=N_NODES)
        return out.reshape(N_NODES, HEAD * OUT_CH)

    def _L1_gnn_ref(features, edge_weights, edges):
        import jax, jax.numpy as jnp
        import numpy as np
        N_NODES = 1250
        N_EDGES = 80000
        FEAT_DIM = 128
        AGG_STRENGTH = 0.3
        EPS = 1e-08
        n_nodes = features.shape[0]
        src = edges[:, 0]
        tgt = edges[:, 1]
        msgs = features[src] * edge_weights[:, None]
        enhanced = jax.ops.segment_sum(msgs, tgt, num_segments=n_nodes)
        counts = jax.ops.segment_sum(edge_weights, tgt, num_segments=n_nodes)
        counts = jnp.maximum(counts, EPS)
        enhanced = enhanced / counts[:, None]
        mask = (counts > EPS).astype(features.dtype)[:, None]
        a = AGG_STRENGTH
        return features * (1.0 - a * mask) + enhanced * (a * mask)
    edge_index_t = jnp.stack([src, dst], axis=1)
    x = _layernorm(x + _L0_gnn_ref(x, L0_gnn_w1, L0_gnn_w2, L0_gnn_a, src, dst), axis=-1)
    x = _layernorm(x + _L1_gnn_ref(x, edge_weight, edge_index_t), axis=-1)
    return x

_drawn_inputs = setup_inputs


def setup_inputs(seed=0):
    import zlib

    import numpy as np

    out = dict(_drawn_inputs(seed))
    spreads = {}
    factors = {}
    for name, (base, spread) in spreads.items():
        noise = np.random.default_rng([zlib.crc32(name.encode()), seed]).standard_normal(out[name].shape)
        drawn = base * np.exp(spread * noise) if base else spread * noise
        out[name] = jnp.asarray(drawn.astype(out[name].dtype))
    for name, factor in factors.items():
        out[name] = (out[name] * factor).astype(out[name].dtype)
    return out
```

```python
import concourse.bass as bass
from concourse import mybir
from contextlib import ExitStack


def graph_kernel(nc, x, src, dst, edge_weight, w1, w2, a, out):
    fp32, bf16, i32 = mybir.dt.float32, mybir.dt.bfloat16, mybir.dt.int32
    ALU, ACT, AX = mybir.AluOpType, mybir.ActivationFunctionType, mybir.AxisListType
    ds = bass.ds

    P = 128
    N, C = x.shape
    E = src.shape[0]
    HEADS, CH = 8, 16
    SLOPE, MIX = 0.3, 0.3
    EPS_COUNT, EPS_NORM = 1e-8, 1e-5
    ET, NT = -(-E // P), -(-N // P)
    K = 16
    NG = -(-(ET + NT - 1) // K)
    NS = NG * K
    SM = NS // P
    NA = NS - ET + 1
    B, J = 4, K // 4
    QW = NS // 4
    FULL_E, TAIL_E = E // P, E % P
    FULL_N, TAIL_N = N // P, N % P
    W0 = C + HEADS
    W1 = C + 1
    SLOTS = K + 1
    BIG = 1e30
    NO_NODE = 1000000
    CT = 7
    NC_ = NT // CT
    assert NS % P == 0 and NT % CT == 0 and K * HEADS == P and TAIL_E and TAIL_N

    def dram(name, shape, dt):
        return nc.dram_tensor(name, shape, dt, kind="Internal").ap()

    edge_rows = dram("edge_rows", [ET, 3 * P], i32)
    hi_rows = dram("hi_rows", [NT * P, C], fp32)
    x1_rows = dram("x1_rows", [NT * P, C], fp32)
    locals_flat = dram("locals_flat", [1 + NS * P], fp32)
    starts_flat = dram("starts_flat", [NS * P + P], fp32)
    through_flat = dram("through_flat", [2, NS], fp32)

    ctx = ExitStack()
    with ctx:
        def sb(name, shape, dt=fp32):
            return ctx.enter_context(nc.sbuf_tensor(name, shape, dt))

        def ps(name, shape=(P, 512), dt=fp32):
            return ctx.enter_context(nc.psum_tensor(name, list(shape), dt))

        def sem(name):
            return ctx.enter_context(nc.semaphore(name))

        iota = sb("iota", [P, NS])
        tile_no = sb("tile_no", [P, SM])
        step_no = sb("step_no", [P, SM])
        ident = sb("ident", [P, P])
        ones_bf = sb("ones_bf", [P, P], bf16)
        a_rep = sb("a_rep", [P, C])
        w12 = sb("w12", [P, 2 * C])
        pads = sb("pads", [1, 3, P], i32)
        eps_col = sb("eps_col", [P, 1])
        last_dst = sb("last_dst", [P, SM], i32)
        last_tile = sb("last_tile", [P, SM], i32)
        ends_at = sb("ends_at", [P, SM])
        passed = sb("passed", [P, 2, NS], bf16)
        edge_tile_row = sb("edge_tile_row", [1, NS])
        node_tile_row = sb("node_tile_row", [1, NS], i32)
        edge_tile_col = sb("edge_tile_col", [P, SM], i32)
        first_node = sb("first_node", [P, SM])
        src_idx = sb("src_idx", [P, NS + K], i32)
        local = sb("local", [P, NS])
        weight = sb("weight", [P, NS])
        x_sb = sb("x_sb", [P, NT, C])
        hj = sb("hj", [P, NA, C])
        acc = sb("acc", [P, NA, W0])
        idx_g = sb("idx_g", [P, 2, K], i32)
        rows = sb("rows", [P, 2 * K, C + 4])
        S = sb("S", [P, 2 * K, P])
        msg = sb("msg", [P, 2, K, W0])
        logits = sb("logits", [P, 2, HEADS, K])
        starts = sb("starts", [P, 2, P + 1])
        through = sb("through", [1, 2, 2, HEADS, SLOTS])
        ST = sb("ST", [P, 2, B * P])
        scaled = sb("scaled", [P, 2, B * P])
        weighted = sb("weighted", [P, B * P])
        scan_a = sb("scan_a", [P, P])
        scan_b = sb("scan_b", [P, P])
        last_max = sb("last_max", [1, HEADS, SLOTS])
        first_max = sb("first_max", [1, HEADS, SLOTS])
        up = sb("up", [1, HEADS, SLOTS])
        down = sb("down", [1, HEADS, SLOTS])
        updown = sb("updown", [1, 2, P])
        shift = sb("shift", [1, 2, HEADS])
        below = sb("below", [P, P])
        rescale = sb("rescale", [P, HEADS])
        fin = sb("fin", [P, 6, CT, HEADS])
        stats = sb("stats", [P, CT, 6])
        mv = sb("mv", [P, CT, 2])
        rstd = sb("rstd", [P, 3, CT])
        tables = msg[:, :, :, :].rearrange("p a k w -> p (a k w)")[:, 0:4 * 3 * P].bitcast(i32) \
            .rearrange("p (m q e) -> p m q e", m=4, q=3)
        tab_f = sb("tab_f", [P, 2, 2, P])
        local_s = S[:, :, :].rearrange("p k n -> p (k n)")[:, 0:SM * P].rearrange("p (m e) -> p m e", m=SM)
        prev_s = S[:, :, :].rearrange("p k n -> p (k n)")[:, SM * P:2 * SM * P].rearrange("p (m e) -> p m e", m=SM)
        small = sb("small", [P, 4, SM])

        psU = [ps("psU0"), ps("psU1")]
        psL = ps("psL")
        psT = ps("psT")
        psP = [ps("psP0"), ps("psP1")]
        psA = ps("psA")
        psB = ps("psB")

        consts, memsets, fills, w_in, x_in, last_in, rows_made, pad_in = map(
            sem, ("consts", "memsets", "fills", "w_in", "x_in", "last_in", "rows_made", "pad_in"))
        pre = sem("pre")
        passed_ready, passed_used, tiles_row, col_ps, col_ready = map(
            sem, ("passed_ready", "passed_used", "tiles_row", "col_ps", "col_ready"))
        table_in = [sem(f"table_in{m}") for m in range(4)]
        tab_ready, tab_ps, tab_out = map(sem, ("tab_ready", "tab_ps", "tab_out"))
        locals_out, prev_in, starts_out, next_in, through_out = map(
            sem, ("locals_out", "prev_in", "starts_out", "next_in", "through_out"))
        starts_made, through_made, next_used = map(sem, ("starts_made", "through_made", "next_used"))
        xT_ps, xT_sb, h_ps, h_sb, hi_out = map(sem, ("xT_ps", "xT_sb", "h_ps", "h_sb", "hi_out"))
        acc_zero = sem("acc_zero")
        node_tiles_ready = sem("node_tiles_ready")
        idx_ready = sem("idx_ready")
        rows_in = [[sem(f"rows_in{p}{j}") for j in range(J)] for p in range(2)]
        flags_in = [sem("flags_in0"), sem("flags_in1")]
        S_ready, ST_ps, ST_sb, U_ready, scaled_ready, leaky_done, weighted_done, logits_ready = map(
            sem, ("S_ready", "ST_ps", "ST_sb", "U_ready", "scaled_ready", "leaky_done",
                  "weighted_done", "logits_ready"))
        logitsT, scan1, scan2, rows_ps, rows_sb, scan_up, updown_ps, scan3, scan4, maxT = map(
            sem, ("logitsT", "scan1", "scan2", "rows_ps", "rows_sb", "scan_up", "updown_ps",
                  "scan3", "scan4", "maxT"))
        updown_sb = sem("updown_sb")
        shift1, shift2, below_ready, weights_ready, rescale_ps, rescale_sb, rescaled = map(
            sem, ("shift1", "shift2", "below_ready", "weights_ready", "rescale_ps", "rescale_sb",
                  "rescaled"))
        msg_ready, sums_ps, added = map(sem, ("msg_ready", "sums_ps", "added"))
        idx1_ready, S1_ready, sums1_ps, added1 = map(sem, ("idx1_ready", "S1_ready", "sums1_ps", "added1"))
        rows1_in = [[sem(f"rows1_in{p}{j}") for j in range(J)] for p in range(2)]
        fin_v = [sem("fin_v0"), sem("fin_v1")]
        fin_var = [sem("fin_var0"), sem("fin_var1")]
        fin_std = [sem("fin_std0"), sem("fin_std1")]
        fin_rs = [sem("fin_rs0"), sem("fin_rs1")]
        fin_x = [sem("fin_x0"), sem("fin_x1")]
        x1_out, out_done, acc1_zero = map(sem, ("x1_out", "out_done", "acc1_zero"))

        passed_by = {e: sem(f"passed_by_{e}") for e in ("pe", "pool", "dve")}

        block = ctx.enter_context(nc.Block())

        def groups(engine, first, pair, last):
            first(0)
            pair(1, 0, 1)
            with engine.Fori(0, NG // 2 - 1) as it:
                r = engine.snap(it + 1)
                for parity in range(2):
                    pair(r * 2 + parity, r, parity)
            last(NG - 1)

        @block.sync
        def _(sp):
            sp.wait_ge(memsets, 3)
            tiles = dst[0:FULL_E * P].rearrange("(i e) -> i e", e=P)[:, P - 1:P]
            whole = FULL_E // SM
            with nc.allow_non_contiguous_dma(reason="one element of each edge tile"):
                sp.dma_start(last_dst[0:whole, :],
                             tiles[0:whole * SM, :].rearrange("(p c) o -> p (c o)", c=SM)).then_inc(last_in, 16)
                sp.dma_start(last_dst[whole:whole + 1, 0:FULL_E - whole * SM],
                             tiles[whole * SM:FULL_E, :].rearrange("(p c) o -> p (c o)", p=1)).then_inc(last_in, 16)
            sp.dma_start(w12[:, 0:C], w1).then_inc(w_in, 16)
            sp.dma_start(w12[:, C:2 * C], w2).then_inc(w_in, 16)
            sp.dma_start(x_sb[:, 0:FULL_N, :], x[0:FULL_N * P, :].rearrange("(t p) c -> p t c", p=P)).then_inc(x_in, 16)
            sp.wait_ge(fills, 6)
            sp.dma_start(x_sb[0:TAIL_N, FULL_N, :], x[FULL_N * P:N, :]).then_inc(x_in, 16)
            sp.dma_start(a_rep[:, :], a.partition_broadcast(P) if len(a.shape) == 1 else a[0, :].partition_broadcast(P)).then_inc(w_in, 16)
            even = FULL_E // 16 * 16
            for q, v in enumerate((src, dst, edge_weight.bitcast(i32))):
                full = v[0:FULL_E * P].rearrange("(i e) -> i e", e=P)
                sp.dma_start(edge_rows[0:even, q * P:q * P + P], full[0:even, :]).then_inc(rows_made, 16)
                sp.dma_start(edge_rows[even:FULL_E, q * P:q * P + P], full[even:FULL_E, :]).then_inc(rows_made, 16)
                sp.dma_start(edge_rows[FULL_E:ET, q * P:q * P + TAIL_E],
                             v[FULL_E * P:E].rearrange("(o e) -> o e", o=1)).then_inc(rows_made, 16)
                sp.dma_start(edge_rows[FULL_E:ET, q * P + TAIL_E:q * P + P], pads[:, q, TAIL_E:P]).then_inc(rows_made, 16)
            sp.wait_ge(h_sb, 2 * NT)
            sp.dma_start(hi_rows.rearrange("(t p) c -> p t c", p=P), acc[:, 0:NT, 0:C]).then_inc(hi_out, 16)
            sp.wait_ge(tab_out, 3 * SM)
            flat = locals_flat[1:1 + NS * P].rearrange("(m p e) -> p m e", p=P, e=P)
            sp.dma_start(locals_flat[0:1].rearrange("(o e) -> o e", o=1), eps_col[0:1, 0:1]).then_inc(locals_out, 16)
            sp.dma_start(flat, local_s).then_inc(locals_out, 16)
            sp.wait_ge(locals_out, 32)
            sp.dma_start(prev_s, locals_flat[0:NS * P].rearrange("(m p e) -> p m e", p=P, e=P)).then_inc(prev_in, 16)
            sp.wait_ge(starts_made, 1)
            sp.dma_start(starts_flat[0:NS * P].rearrange("(m p e) -> p m e", p=P, e=P), prev_s).then_inc(starts_out, 16)
            sp.dma_start(starts_flat[NS * P:NS * P + 1].rearrange("(o e) -> o e", o=1), small[0:1, 3, 0:1]).then_inc(starts_out, 16)
            sp.wait_ge(starts_out, 32)
            with nc.allow_non_contiguous_dma(reason="one element of each step"):
                sp.dma_start(small[:, 0, :].rearrange("p (m o) -> p m o", o=1),
                             starts_flat[P:P + NS * P].rearrange("(m p e) -> p m e", p=P, e=P)[:, :, 0:1]).then_inc(next_in, 16)
                sp.wait_ge(through_made, 2)
                sp.dma_start(through_flat[0, :].rearrange("(m p) -> p m", p=P), small[:, 1, :]).then_inc(through_out, 16)
                sp.dma_start(through_flat[1, :].rearrange("(m p) -> p m", p=P), small[:, 2, :]).then_inc(through_out, 16)
            sp.wait_ge(through_out, 32)

            def flags(g, parity):
                for h in range(HEADS):
                    part = starts_flat[ds(g * (K * P), K * P + P)]
                    sp.dma_start(starts[h * K:h * K + K, parity, 0:P], part[0:K * P].rearrange("(k e) -> k e", e=P)) \
                        .then_inc(flags_in[parity], 16)
                    sp.dma_start(starts[h * K:h * K + K, parity, P:P + 1],
                                 part[P:K * P + P].rearrange("(k e) -> k e", e=P)[:, 0:1]).then_inc(flags_in[parity], 16)
                for d in range(2):
                    sp.dma_start(through[0:1, parity, d, :, 1 - d:1 - d + K],
                                 through_flat[d:d + 1, ds(g * K, K)].rearrange("o (b k) -> o b k", b=1).to_broadcast([1, HEADS, K])) \
                        .then_inc(flags_in[parity], 16)

            with nc.allow_non_contiguous_dma(reason="the next tile's first element"):
                flags(0, 0)
                flags(1, 1)
                with sp.Fori(0, NG // 2 - 1) as it:
                    r = sp.snap(it + 1)
                    for parity in range(2):
                        sp.wait_ge(scan4, r * 2 + (parity - 1))
                        flags(r * 2 + parity, parity)

            sp.wait_ge(fin_x[0], NT)
            sp.dma_start(x1_rows.rearrange("(t p) c -> p t c", p=P), x_sb[:, :, :]).then_inc(x1_out, 16)
            whole = FULL_N // CT
            with sp.Fori(0, whole) as c:
                sp.wait_ge(fin_x[1], c * CT + CT)
                sp.dma_start(out[ds(c * (CT * P), CT * P), :].rearrange("(t p) c -> p t c", p=P),
                             x_sb[:, ds(c * CT, CT), :]).then_inc(out_done, 16)
            sp.wait_ge(fin_x[1], NT)
            n = 0
            if FULL_N > whole * CT:
                sp.dma_start(out[whole * CT * P:FULL_N * P, :].rearrange("(t p) c -> p t c", p=P),
                             x_sb[:, whole * CT:FULL_N, :]).then_inc(out_done, 16)
                n = 1
            sp.dma_start(out[FULL_N * P:N, :], x_sb[0:TAIL_N, FULL_N, :]).then_inc(out_done, 16)
            sp.wait_ge(out_done, 16 * (whole + n + 1))

        @block.gpsimd
        def _(pool):
            pool.memset(last_dst[:, :], NO_NODE).then_inc(memsets, 1)
            pool.memset(pads[:, :, :], 0).then_inc(memsets, 1)
            pool.wait_ge(memsets, 2)
            pool.memset(pads[:, 1, :], NO_NODE).then_inc(memsets, 1)
            pool.iota(iota[:, :], [[1, NS]], base=0, channel_multiplier=0,
                      allow_small_or_imprecise_dtypes=True).then_inc(consts, 1)
            pool.iota(tile_no[:, :], [[1, SM]], base=0, channel_multiplier=SM,
                      allow_small_or_imprecise_dtypes=True).then_inc(consts, 1)
            pool.iota(step_no[:, :], [[P, SM]], base=0, channel_multiplier=1,
                      allow_small_or_imprecise_dtypes=True).then_inc(consts, 1)
            pool.memset(ones_bf[:, :], 1.0).then_inc(consts, 1)
            pool.memset(ident[:, :], 0.0).then_inc(consts, 1)
            pool.wait_ge(consts, 5)
            pool.affine_select(out=ident[:, :], in_=ident[:, :], compare_op=ALU.not_equal, fill=1.0,
                               base=0, pattern=[[-1, P]], channel_multiplier=1).then_inc(consts, 1)
            pool.wait_ge(rows_made, 16 * 12)
            pool.wait_ge(col_ready, 1)
            for m in range(SM):
                if m >= 4:
                    pool.wait_ge(tab_out, 3 * (m - 3))
                pool.indirect_dma_start(tables[:, m % 4, :, :].rearrange("p q e -> p (q e)"), None, edge_rows,
                                        bass.IndirectOffsetOnAxis(ap=edge_tile_col[:, m:m + 1], axis=0)) \
                    .then_inc(table_in[m % 4], 16)

            def gather(table, arrived, parity):
                for j in range(J):
                    yield j
                    for k in range(j * B, j * B + B):
                        pool.indirect_dma_start(rows[:, parity * K + k, 0:C], None, table,
                                                bass.IndirectOffsetOnAxis(ap=idx_g[:, parity, k:k + 1], axis=0)) \
                            .then_inc(arrived[parity][j], 16)

            pool.wait_ge(hi_out, 16)
            for table, arrived, ready, used in ((hi_rows, rows_in, idx_ready, msg_ready),
                                                (x1_rows, rows1_in, idx1_ready, sums1_ps)):
                per = J if used is msg_ready else 2 * J
                if table is x1_rows:
                    pool.wait_ge(x1_out, 16)
                for g in range(2):
                    pool.wait_ge(ready, g + 1)
                    for j in gather(table, arrived, g):
                        pass
                with pool.Fori(0, NG // 2 - 1) as it:
                    r = pool.snap(it + 1)
                    for parity in range(2):
                        pool.wait_ge(ready, r * 2 + (parity + 1))
                        for j in gather(table, arrived, parity):
                            pool.wait_ge(used, r * (2 * per) + ((parity - 2) * per + (j + 1) * (per // J)))
                            pool.sem_inc(passed_by["pool"], 1)

        @block.tensor
        def _(pe):
            pe.wait_ge(consts, 6)
            quarters = [psU[0], psU[1], psL, psT]
            for c in range(SM):
                pe.wait_ge(passed_ready, c + 1)
                for q in range(4):
                    mm = pe.matmul(quarters[q][:, 0:QW], ones_bf[:, :], passed[:, c % 2, q * QW:(q + 1) * QW],
                                   start=(c == 0), stop=(c == SM - 1))
                mm.then_inc(passed_used, 1)
            pe.wait_ge(tiles_row, 4)
            for m in range(SM):
                tr = pe.transpose(psA[:, m:m + 1], edge_tile_row[0:1, m * P:m * P + P], ident[0:1, 0:1])
            tr.then_inc(col_ps, 1)
            pe.wait_ge(x_in, 32)
            pe.wait_ge(w_in, 48)
            pe.wait_ge(fills, 1)
            for t in range(NT):
                if t >= 2:
                    pe.wait_ge(xT_sb, t - 1)
                pe.transpose(psP[t % 2][:, 0:P], x_sb[:, t, :], ident[:, :]).then_inc(xT_ps, 1)
                pe.wait_ge(xT_sb, t + 1)
                if t >= 2:
                    pe.wait_ge(h_sb, 2 * (t - 1))
                pe.matmul(psU[t % 2][:, 0:2 * C], ST[:, t % 2, 0:P], w12[:, :], start=True, stop=True).then_inc(h_ps, 1)
            for m in range(SM):
                pe.wait_ge(tab_ready, 2 * m + 2)
                pe.wait_ge(table_in[m % 4], 16 * (m // 4 + 1))
                if m >= 1:
                    pe.wait_ge(tab_out, 3 * m)
                pe.transpose(psT[:, 0:P], tab_f[:, m % 2, 0, :], ident[:, :])
                pe.transpose(psT[:, P:2 * P], local_s[:, m, :], ident[:, :])
                pe.transpose(psT[:, 2 * P:3 * P], tables[:, m % 4, 2, :].bitcast(fp32), ident[:, :]).then_inc(tab_ps, 1)

            def batch(g, r, parity, j):
                b = g * J + j
                s0 = parity * K + j * B
                pe.wait_ge(S_ready, b + 1)
                if not (isinstance(g, int) and g * J + j == 0):
                    pe.wait_ge(ST_sb, b)
                for k in range(B):
                    tr = pe.transpose(psT[:, k * P:k * P + P], S[:, s0 + k, :], ident[:, :])
                tr.then_inc(ST_ps, 1)
                pe.wait_ge(rows_in[parity][j], (r + 1) * (16 * B))
                if not (isinstance(g, int) and g * J + j < 2):
                    pe.wait_ge(leaky_done, b - 1)
                U = psU[j % 2]
                pe.matmul(U[:, :], ident[:, :], rows[:, s0:s0 + B, 0:C], start=True, stop=True, skip_group_check=True)
                pe.wait_ge(ST_sb, b + 1)
                for k in range(B):
                    mm = pe.matmul(U[:, k * P:k * P + P], ST[:, j % 2, k * P:k * P + P], hj[:, ds(tile_of[j * B + k], 1), :],
                                   start=False, stop=True, skip_group_check=True)
                mm.then_inc(U_ready, 1)

            tile_of = [0] * K

            def node_tiles(g):
                _, values = nc.values_load_multi_w_load_instructions(
                    node_tile_row[0:1, ds(g * K, K)], [mybir.EngineType.PE], min_val=0, max_val=NA - 1,
                    skip_runtime_bounds_check_because="a step's node tile is at most NS - ET")
                tile_of[:] = values

            def chain(q, parity):
                pe.wait_ge(logits_ready, q * J + J)
                if not (isinstance(q, int) and q == 0):
                    pe.wait_ge(below_ready, q)
                pe.transpose(psA[:, 0:P], logits[:, parity, :, :].rearrange("p h k -> p (h k)"), ident[:, :]).then_inc(logitsT, 1)
                pe.wait_ge(scan2, q + 1)
                if not (isinstance(q, int) and q == 0):
                    pe.wait_ge(rescale_sb, q)
                pe.transpose(psB[0:1, 0:P], scan_b[:, P - 1:P], ident[:, :])
                pe.transpose(psB[0:1, P:2 * P], scan_b[:, 0:1], ident[:, :]).then_inc(rows_ps, 1)
                pe.wait_ge(updown_sb, q * 2 + 2)
                pe.sem_inc(passed_by["pe"], 1)
                pe.transpose(psB[:, 256:257], updown[0:1, 0, :], ident[0:1, 0:1])
                pe.transpose(psB[:, 257:258], updown[0:1, 1, :], ident[0:1, 0:1]).then_inc(updown_ps, 1)
                pe.wait_ge(scan4, q + 1)
                pe.transpose(psA[:, P:2 * P], scan_b[:, :], ident[:, :]).then_inc(maxT, 1)
                pe.wait_ge(shift2, q + 1)
                pe.matmul(psB[:, 264:264 + HEADS], S[0:1, parity * K, :], shift[0:1, 1, :], start=True, stop=True) \
                    .then_inc(rescale_ps, 1)

            def sums(q, parity, j):
                pe.wait_ge(msg_ready, q * J + (j + 1))
                for i in range(2):
                    n = (q * J + j) * 2 + i
                    if not (isinstance(q, int) and q == 0 and j == 0):
                        pe.wait_ge(added, n * 2 - 2)
                    for e in range(2):
                        k = j * B + i * 2 + e
                        mm = pe.matmul(psP[i][:, e * 256:e * 256 + W0], S[:, parity * K + k, :], msg[:, parity, k, :],
                                       start=True, stop=True)
                    mm.then_inc(sums_ps, 1)

            def first(g):
                pe.wait_ge(node_tiles_ready, 1)
                pe.wait_ge(h_sb, 2 * NT)
                pe.wait_ge(fills, 6)
                node_tiles(g)
                for j in range(J):
                    batch(g, 0, 0, j)

            def pair(g, r, parity):
                node_tiles(g)
                chain(g - 1, 1 - parity)
                for j in range(J):
                    batch(g, r, parity, j)
                    sums(g - 1, 1 - parity, j)

            def last(q):
                chain(q, 1)
                for j in range(J):
                    sums(q, 1, j)

            groups(pe, first, pair, last)

            def sums1(g, r, parity):
                for j in range(J):
                    pe.wait_ge(rows1_in[parity][j], (r + 1) * (16 * B))
                    pe.wait_ge(S1_ready, g * J + (j + 1))
                    for i in range(2):
                        n = (g * J + j) * 2 + i
                        if not (isinstance(g, int) and g == 0 and j == 0):
                            pe.wait_ge(added1, n * 2 - 2)
                        for e in range(2):
                            k = parity * K + j * B + i * 2 + e
                            mm = pe.matmul(psP[i][:, e * 256:e * 256 + W1], S[:, k, :], rows[:, k, 0:W1],
                                           start=True, stop=True)
                        mm.then_inc(sums1_ps, 1)

            pe.wait_ge(acc1_zero, 2)
            groups(pe, lambda g: sums1(g, 0, 0), sums1, lambda q: None)

        @block.scalar
        def _(act):
            for t in range(NT):
                act.wait_ge(xT_ps, t + 1)
                if t >= 2:
                    act.wait_ge(h_ps, t - 1)
                act.activation(ST[:, t % 2, 0:P], psP[t % 2][:, 0:P], ACT.Copy).then_inc(xT_sb, 1)
                act.wait_ge(h_ps, t + 1)
                act.activation(acc[:, t, 0:C], psU[t % 2][:, 0:C], ACT.Copy).then_inc(h_sb, 1)
                act.activation(hj[:, t, :], psU[t % 2][:, C:2 * C], ACT.Copy).then_inc(h_sb, 1)

            def batch(g, j):
                b = g * J + j
                early = isinstance(g, int) and g * J + j < 2
                act.wait_ge(ST_ps, b + 1)
                if not early:
                    act.wait_ge(U_ready, b - 1)
                act.activation(ST[:, j % 2, :], psT[:, :], ACT.Copy).then_inc(ST_sb, 1)
                act.wait_ge(U_ready, b + 1)
                if not early:
                    act.wait_ge(leaky_done, b - 1)
                act.activation(scaled[:, j % 2, :], psU[j % 2][:, :], ACT.Copy, scale=SLOPE).then_inc(scaled_ready, 1)

            def exps(q, parity):
                if not (isinstance(q, int) and q < 2):
                    act.wait_ge(sums_ps, q * (2 * J) - 2 * J)
                act.wait_ge(below_ready, q + 1)
                act.activation(msg[:, parity, :, C:W0].rearrange("p k h -> p h k"),
                               below[:, :].rearrange("p (h k) -> p h k", k=K), ACT.Exp).then_inc(weights_ready, 1)
                act.wait_ge(rescale_ps, q + 1)
                if not (isinstance(q, int) and q == 0):
                    act.wait_ge(rescaled, q * 2)
                act.activation(rescale[:, :], psB[:, 264:264 + HEADS], ACT.Exp).then_inc(rescale_sb, 1)

            def pair(g, r, parity):
                exps(g - 1, 1 - parity)
                for j in range(J):
                    batch(g, j)

            groups(act, lambda g: [batch(g, j) for j in range(J)], pair, lambda q: exps(q, 1))

            def normalise(rnd):
                with act.Fori(0, NC_) as c:
                    act.wait_ge(fin_var[rnd], c + 1)
                    act.activation(rstd[:, 0, :], mv[:, :, 1], ACT.Sqrt, bias=eps_col[:, :]).then_inc(fin_std[rnd], 1)
                    act.wait_ge(fin_rs[rnd], c + 1)
                    for i in range(CT):
                        xt = x_sb[:, ds(c * CT + i, 1), :]
                        act.activation(xt, xt, ACT.Identity, bias=rstd[:, 2, i:i + 1], scale=rstd[:, 1, i:i + 1]) \
                            .then_inc(fin_x[rnd], 1)

            normalise(0)
            normalise(1)

        @block.vector
        def _(dve):
            dve.memset(x_sb[:, FULL_N:NT, :], 0.0).then_inc(fills, 1)
            dve.memset(eps_col[:, :], EPS_NORM).then_inc(fills, 1)
            dve.memset(hj[:, NT:NA, :], 0.0).then_inc(fills, 1)
            dve.memset(small[:, 3, :], -BIG).then_inc(fills, 1)
            dve.memset(src_idx[:, NS:NS + K], 0).then_inc(fills, 1)
            dve.memset(through[:, :, :, :, :], -BIG).then_inc(fills, 1)
            dve.wait_ge(last_in, 32)
            dve.wait_ge(consts, 6)
            dve.tensor_scalar(last_tile[:, :], last_dst[:, :], P.bit_length() - 1, None, ALU.logical_shift_right).then_inc(pre, 1)
            dve.wait_ge(pre, 1)
            dve.tensor_tensor(ends_at[:, :], last_tile[:, :], tile_no[:, :], ALU.add).then_inc(pre, 1)
            dve.wait_ge(pre, 2)
            for c in range(SM):
                if c >= 2:
                    dve.wait_ge(passed_used, c - 1)
                dve.tensor_scalar(passed[:, c % 2, :], iota[:, :], ends_at[:, c:c + 1], None, ALU.is_gt).then_inc(passed_ready, 1)
            dve.wait_ge(passed_used, SM)
            for q, bank in enumerate((psU[0], psU[1], psL, psT)):
                dve.tensor_copy(edge_tile_row[:, q * QW:(q + 1) * QW], bank[0:1, 0:QW]).then_inc(tiles_row, 1)
            dve.wait_ge(tiles_row, 4)
            dve.tensor_tensor(node_tile_row[:, :], iota[0:1, :], edge_tile_row[:, :], ALU.subtract).then_inc(node_tiles_ready, 1)
            dve.wait_ge(col_ps, 1)
            dve.tensor_copy(edge_tile_col[:, :], psA[:, 0:SM]).then_inc(col_ready, 1)
            dve.tensor_tensor(first_node[:, :], step_no[:, :], psA[:, 0:SM], ALU.subtract).then_inc(pre, 1)
            dve.wait_ge(pre, 3)
            dve.tensor_scalar(first_node[:, :], first_node[:, :], float(P), None, ALU.mult).then_inc(pre, 1)
            dve.wait_ge(pre, 4)
            for m in range(SM):
                dve.wait_ge(table_in[m % 4], 16 * (m // 4 + 1))
                dve.tensor_copy(tab_f[:, m % 2, 0, :], tables[:, m % 4, 0, :]).then_inc(tab_ready, 1)
                dve.tensor_scalar(local_s[:, m, :], tables[:, m % 4, 1, :], first_node[:, m:m + 1], None,
                                  ALU.subtract).then_inc(tab_ready, 1)
                dve.wait_ge(tab_ps, m + 1)
                for q, table in enumerate((src_idx, local, weight)):
                    dve.tensor_copy(table[:, m * P:m * P + P], psT[:, q * P:q * P + P]).then_inc(tab_out, 1)
            dve.wait_ge(prev_in, 16)
            dve.tensor_tensor(prev_s, local_s, prev_s, ALU.not_equal).then_inc(pre, 1)
            dve.wait_ge(pre, 5)
            dve.tensor_scalar(prev_s, prev_s, -BIG, None, ALU.mult).then_inc(starts_made, 1)
            dve.wait_ge(starts_made, 1)
            dve.tensor_reduce(first_node[:, :], prev_s[:, :, 1:P], AX.X, ALU.min).then_inc(pre, 1)
            dve.wait_ge(pre, 6)
            dve.tensor_tensor(small[:, 1, :], first_node[:, :], prev_s[:, :, 0], ALU.add).then_inc(through_made, 1)
            dve.wait_ge(next_in, 16)
            dve.tensor_tensor(small[:, 2, :], first_node[:, :], small[:, 0, :], ALU.add).then_inc(through_made, 1)
            dve.wait_ge(hi_out, 16)
            dve.memset(acc[:, :, :], 0.0).then_inc(acc_zero, 1)
            dve.memset(up[:, :, :], -BIG).then_inc(acc_zero, 1)
            dve.memset(first_max[:, :, :], -BIG).then_inc(acc_zero, 1)
            dve.wait_ge(acc_zero, 3)
            dve.wait_ge(node_tiles_ready, 1)
            dve.wait_ge(starts_out, 32)

            def next_idx(g, parity, ready):
                dve.tensor_copy(idx_g[:, parity, :], src_idx[:, ds(g * K, K)]).then_inc(ready, 1)

            local_g = sb("local_g", [P, 2, K])
            weight_g = sb("weight_g", [P, 2, K])
            local_ready = sem("local_ready")

            def onehot(g, parity, j):
                if not (isinstance(g, int) and g < 2):
                    dve.wait_ge(sums_ps, g * (2 * J) + (2 * (j + 1) - 4 * J))
                for k in range(j * B, j * B + B):
                    op = dve.tensor_scalar(S[:, parity * K + k, :], iota[:, 0:P], local_g[:, parity, k:k + 1], None, ALU.is_equal)
                op.then_inc(S_ready, 1)

            def batch(g, parity, j):
                b = g * J + j
                dve.wait_ge(scaled_ready, b + 1)
                dve.tensor_tensor(psL[:, :], psU[j % 2][:, :], scaled[:, j % 2, :], ALU.max).then_inc(leaky_done, 1)
                dve.wait_ge(leaky_done, b + 1)
                dve.tensor_tensor(weighted[:, :].rearrange("p (k c) -> p k c", k=B), psL[:, :].rearrange("p (k c) -> p k c", k=B),
                                  a_rep[:, :].rearrange("p (o c) -> p o c", o=1).to_broadcast([P, B, C]), ALU.mult).then_inc(weighted_done, 1)
                dve.wait_ge(weighted_done, b + 1)
                dve.tensor_reduce(logits[:, parity, :, j * B:j * B + B].rearrange("p h k -> p k h"),
                                  weighted[:, :].rearrange("p (k h c) -> p k h c", k=B, h=HEADS), AX.X, ALU.add) \
                    .then_inc(logits_ready, 1)

            def chain(q, r, parity):
                st, nx = starts[:, parity, 0:P], starts[:, parity, 1:P + 1][:, ::-1]
                thr, back = through[0:1, parity, 0], through[0:1, parity, 1]
                flat = lambda t: t.rearrange("o h s -> o (h s)")
                dve.wait_ge(flags_in[parity], (r + 1) * (16 * (2 * HEADS + 2)))
                dve.wait_ge(logitsT, q + 1)
                dve.tensor_tensor_scan(scan_a[:, :], st, psA[:, 0:P], -BIG, ALU.add, ALU.max).then_inc(scan1, 1)
                dve.wait_ge(scan1, q + 1)
                dve.tensor_tensor_scan(scan_b[:, ::-1], nx, scan_a[:, ::-1], -BIG, ALU.add, ALU.max).then_inc(scan2, 1)
                dve.wait_ge(rows_ps, q + 1)
                dve.tensor_copy(last_max[:, :, 0:1], up[:, :, K:SLOTS]).then_inc(rows_sb, 1)
                dve.tensor_copy(last_max[:, :, 1:SLOTS], psB[0:1, 0:P].rearrange("o (h k) -> o h k", k=K)).then_inc(rows_sb, 1)
                dve.tensor_copy(first_max[:, :, 0:K], psB[0:1, P:2 * P].rearrange("o (h k) -> o h k", k=K)).then_inc(rows_sb, 1)
                dve.wait_ge(rows_sb, q * 3 + 3)
                dve.tensor_tensor_scan(flat(up[:, :, :]), flat(thr), flat(last_max[:, :, :]), -BIG, ALU.add, ALU.max).then_inc(scan_up, 1)
                dve.tensor_tensor_scan(flat(down[:, :, :])[:, ::-1], flat(back)[:, ::-1], flat(first_max[:, :, :])[:, ::-1], -BIG,
                                       ALU.add, ALU.max).then_inc(scan_up, 1)
                dve.wait_ge(scan_up, q * 2 + 2)
                dve.tensor_copy(updown[:, 0, :].rearrange("o (h k) -> o h k", k=K), up[:, :, 0:K]).then_inc(updown_sb, 1)
                dve.tensor_copy(updown[:, 1, :].rearrange("o (h k) -> o h k", k=K), down[:, :, 1:SLOTS]).then_inc(updown_sb, 1)
                dve.wait_ge(updown_ps, q + 1)
                dve.tensor_tensor_scan(scan_a[:, :], st, psA[:, 0:P], psB[:, 256:257], ALU.add, ALU.max).then_inc(scan3, 1)
                dve.wait_ge(scan3, q + 1)
                dve.tensor_tensor_scan(scan_b[:, ::-1], nx, scan_a[:, ::-1], psB[:, 257:258], ALU.add, ALU.max).then_inc(scan4, 1)
                dve.wait_ge(maxT, q + 1)
                dve.tensor_tensor(shift[:, 0, :], last_max[:, :, 0], psA[0:1, P:2 * P].rearrange("o (h k) -> o h k", k=K)[:, :, 0],
                                  ALU.subtract).then_inc(shift1, 1)
                dve.wait_ge(shift1, q + 1)
                dve.tensor_scalar(shift[:, 1, :], shift[:, 0, :], 0.0, None, ALU.min).then_inc(shift2, 1)
                if not (isinstance(q, int) and q == 0):
                    dve.wait_ge(weights_ready, q)
                dve.tensor_tensor(below[:, :], logits[:, parity, :, :].rearrange("p h k -> p (h k)"), psA[:, P:2 * P],
                                  ALU.subtract).then_inc(below_ready, 1)

            tile_of = [0] * K

            def node_tiles(g):
                _, values = nc.values_load_multi_w_load_instructions(
                    node_tile_row[0:1, ds(g * K, K)], [mybir.EngineType.DVE], min_val=0, max_val=NA - 1,
                    skip_runtime_bounds_check_because="a step's node tile is at most NS - ET")
                tile_of[:] = values

            def scale_first(q):
                dve.wait_ge(rescale_sb, q + 1)
                if not (isinstance(q, int) and q == 0):
                    dve.wait_ge(added, q * K)
                num = acc[:, ds(tile_of[0], 1), 0:C].rearrange("p o (h c) -> p (o h) c", h=HEADS)
                den = acc[:, ds(tile_of[0], 1), C:W0].rearrange("p o h -> p (o h)")
                dve.tensor_tensor(num, num, rescale[:, :].rearrange("p (h o) -> p h o", o=1).to_broadcast([P, HEADS, CH]),
                                  ALU.mult).then_inc(rescaled, 1)
                dve.tensor_tensor(den, den, rescale[:, :], ALU.mult).then_inc(rescaled, 1)

            def messages(q, parity, j):
                dve.wait_ge(weights_ready, q + 1)
                s0 = parity * K + j * B
                dve.tensor_tensor(msg[:, parity, j * B:j * B + B, 0:C].rearrange("p k (h c) -> p k h c", h=HEADS),
                                  rows[:, s0:s0 + B, 0:C].rearrange("p k (h c) -> p k h c", h=HEADS),
                                  msg[:, parity, j * B:j * B + B, C:W0].rearrange("p k (h o) -> p k h o", o=1).to_broadcast([P, B, HEADS, CH]),
                                  ALU.mult).then_inc(msg_ready, 1)

            def add(q, j, width, summed, done):
                for i in range(2):
                    n = (q * J + j) * 2 + i
                    dve.wait_ge(summed, n + 1)
                    for e in range(2):
                        if not (isinstance(q, int) and q * J + j + i + e == 0):
                            dve.wait_ge(done, n * 2 + e)
                        k = j * B + i * 2 + e
                        at = acc[:, ds(tile_of[k], 1), 0:width].rearrange("p o w -> p (o w)")
                        dve.tensor_tensor(at, at, psP[i][:, e * 256:e * 256 + width], ALU.add).then_inc(done, 1)

            def first(g):
                dve.wait_ge(tab_out, 3 * SM)
                next_idx(0, 0, idx_ready)
                next_idx(1, 1, idx_ready)
                dve.tensor_copy(local_g[:, 0, :], local[:, 0:K]).then_inc(local_ready, 1)
                dve.wait_ge(local_ready, 1)
                for j in range(J):
                    onehot(0, 0, j)
                    batch(0, 0, j)

            def pair(g, r, parity):
                q, before = g - 1, 1 - parity
                next_idx(g + 1, before, idx_ready)
                dve.tensor_copy(local_g[:, parity, :], local[:, ds(g * K, K)]).then_inc(local_ready, 1)
                dve.wait_ge(local_ready, g + 1)
                node_tiles(q)
                chain(q, r - 1 if parity == 0 else r, before) if not isinstance(g, int) else chain(q, q // 2, before)
                onehot(g, parity, 0)
                batch(g, parity, 0)
                scale_first(q)
                dve.wait_ge(rescaled, q * 2 + 2)
                for j in range(J):
                    messages(q, before, j)
                    if j + 1 < J:
                        onehot(g, parity, j + 1)
                    add(q, j, W0, sums_ps, added)
                    if j + 1 < J:
                        batch(g, parity, j + 1)

            def last(q):
                node_tiles(q)
                chain(q, q // 2, 1)
                scale_first(q)
                dve.wait_ge(rescaled, q * 2 + 2)
                for j in range(J):
                    messages(q, 1, j)
                    add(q, j, W0, sums_ps, added)

            groups(dve, first, pair, last)

            work = msg[:, :, :, :].rearrange("p a k w -> p (a k w)")[:, 0:CT * C].rearrange("p (t c) -> p t c", t=CT)

            def final(rnd):
                v = fin_v[rnd]
                ops = 4 if rnd == 0 else 7
                with dve.Fori(0, NC_) as c:
                    base = dve.snap(c * (ops + 2 * CT + 1))
                    tiles = ds(c * CT, CT)
                    if rnd == 0:
                        dve.tensor_scalar(fin[:, 0], acc[:, tiles, C:W0], 1e-30, None, ALU.max).then_inc(v, 1)
                        dve.wait_ge(v, base + 1)
                        dve.reciprocal(fin[:, 1], fin[:, 0]).then_inc(v, 1)
                        dve.wait_ge(v, base + 2)
                        dve.tensor_tensor(work.rearrange("p t (h c) -> p t h c", h=HEADS),
                                          acc[:, tiles, 0:C].rearrange("p t (h c) -> p t h c", h=HEADS),
                                          fin[:, 1].rearrange("p t (h o) -> p t h o", o=1).to_broadcast([P, CT, HEADS, CH]),
                                          ALU.mult).then_inc(v, 1)
                        dve.wait_ge(v, base + 3)
                        dve.tensor_tensor(x_sb[:, tiles, :], x_sb[:, tiles, :], work, ALU.add).then_inc(v, 1)
                    else:
                        count = acc[:, tiles, C]
                        keep, part, inverse, share = fin[:, 3, :, 0], fin[:, 1, :, 0], fin[:, 2, :, 0], fin[:, 4, :, 0]
                        dve.tensor_scalar(fin[:, 0, :, 0], count, EPS_COUNT, None, ALU.max).then_inc(v, 1)
                        dve.tensor_scalar(part, count, EPS_COUNT, MIX, ALU.is_gt, ALU.mult).then_inc(v, 1)
                        dve.wait_ge(v, base + 2)
                        dve.reciprocal(inverse, fin[:, 0, :, 0]).then_inc(v, 1)
                        dve.tensor_scalar(keep, part, -1.0, 2.0, ALU.mult, ALU.add).then_inc(v, 1)
                        dve.wait_ge(v, base + 4)
                        dve.tensor_tensor(share, inverse, part, ALU.mult).then_inc(v, 1)
                        dve.wait_ge(v, base + 5)
                        dve.tensor_tensor(work, acc[:, tiles, 0:C], fin[:, 4, :, 0:1].to_broadcast([P, CT, C]), ALU.mult).then_inc(v, 1)
                        dve.wait_ge(v, base + 6)
                        for i in range(CT):
                            xt = x_sb[:, ds(c * CT + i, 1), :].rearrange("p o c -> p (o c)")
                            op = dve.scalar_tensor_tensor(out=xt, in0=xt, scalar=fin[:, 3, i, 0:1], in1=work[:, i, :],
                                                          op0=ALU.mult, op1=ALU.add)
                        op.then_inc(v, 1)
                    dve.wait_ge(v, base + ops)
                    dve.sem_inc(passed_by["dve"], 1)
                    for i in range(CT):
                        dve.bn_stats(stats[:, i, :], x_sb[:, ds(c * CT + i, 1), :].rearrange("p o c -> p (o c)")).then_inc(v, 1)
                    dve.wait_ge(v, base + (ops + CT))
                    dve.wait_ge(fin_x[rnd], c * CT)
                    dve.sem_inc(passed_by["dve"], 1)
                    for i in range(CT):
                        op = dve.bn_aggr(mv[:, i, :], stats[:, i, :])
                        if i < CT - 1:
                            op.then_inc(v, 1)
                    op.then_inc(fin_var[rnd], 1)
                    dve.wait_ge(fin_std[rnd], c + 1)
                    dve.reciprocal(rstd[:, 1, :], rstd[:, 0, :]).then_inc(v, 2)
                    dve.wait_ge(v, base + (ops + 2 * CT + 1))
                    dve.scalar_tensor_tensor(out=rstd[:, 2, :], in0=mv[:, :, 0], scalar=-1.0, in1=rstd[:, 1, :],
                                             op0=ALU.mult, op1=ALU.mult).then_inc(fin_rs[rnd], 1)

            dve.wait_ge(added, NS)
            final(0)

            dve.memset(acc[:, :, :], 0.0).then_inc(acc1_zero, 1)
            dve.memset(rows[:, :, C:C + 1], 1.0).then_inc(acc1_zero, 1)
            dve.wait_ge(acc1_zero, 2)
            local1_ready = sem("local1_ready")

            def onehot1(g, parity, j):
                if not (isinstance(g, int) and g < 2):
                    dve.wait_ge(sums1_ps, g * (2 * J) + (2 * (j + 1) - 4 * J))
                for k in range(j * B, j * B + B):
                    op = dve.tensor_scalar(S[:, parity * K + k, :], iota[:, 0:P], local_g[:, parity, k:k + 1],
                                           weight_g[:, parity, k:k + 1], ALU.is_equal, ALU.mult)
                op.then_inc(S1_ready, 1)

            def group1(g, r, parity):
                next_idx(g + 1, 1 - parity, idx1_ready)
                dve.tensor_copy(local_g[:, parity, :], local[:, ds(g * K, K)]).then_inc(local1_ready, 1)
                dve.tensor_copy(weight_g[:, parity, :], weight[:, ds(g * K, K)]).then_inc(local1_ready, 1)
                dve.wait_ge(local1_ready, g * 2 + 2)
                node_tiles(g)
                for j in range(J):
                    onehot1(g, parity, j)
                for j in range(J):
                    add(g, j, W1, sums1_ps, added1)

            next_idx(0, 0, idx1_ready)
            groups(dve, lambda g: group1(g, 0, 0), group1, lambda q: None)
            dve.wait_ge(added1, NS)
            final(1)


_INS = ["x", "src", "dst", "edge_weight", "L0_gnn_w1", "L0_gnn_w2", "L0_gnn_a"]


def kernel(**inputs):
    import numpy as _np
    import concourse.bacc as _bacc
    from concourse import mybir as _mybir
    from concourse.bass_utils import run_bass_kernel_spmd as _run

    nc = _bacc.Bacc("TRN2", target_bir_lowering=False, num_devices=1)
    arrays, args = {}, []
    for name in _INS:
        v = _np.ascontiguousarray(inputs[name])
        arrays[f"in_{name}"] = v
        args.append(nc.dram_tensor(f"in_{name}", v.shape, _mybir.dt.from_np(v.dtype), kind="ExternalInput").ap())
    args.append(nc.dram_tensor("out_0", inputs["x"].shape, _mybir.dt.float32, kind="ExternalOutput").ap())
    graph_kernel(nc, *args)
    r = _run(nc, [arrays], core_ids=[0])
    return r.results[0]["out_0"]
```

```python
import concourse.bass as bass
from concourse import mybir
from contextlib import ExitStack


def graph_kernel(nc, x, src, dst, edge_weight, w1, w2, a, out):
    fp32, bf16, i32, i16 = mybir.dt.float32, mybir.dt.bfloat16, mybir.dt.int32, mybir.dt.int16
    ALU, ACT, AX = mybir.AluOpType, mybir.ActivationFunctionType, mybir.AxisListType
    ds = bass.ds

    P = 128
    N, C = x.shape
    E = src.shape[0]
    HEADS, CH = 8, 16
    SLOPE, MIX = 0.3, 0.3
    EPS_COUNT, EPS_NORM = 1e-8, 1e-5
    ET, NT = -(-E // P), -(-N // P)
    K = 16
    NG = -(-(ET + NT - 1) // K)
    NS = NG * K
    SM = NS // P
    NA = NT + 1
    B, J = 4, K // 4
    RING = 4
    QW = NS // 4
    FULL_E, TAIL_E = E // P, E % P
    FULL_N, TAIL_N = N // P, N % P
    WX = C + HEADS
    W1 = C + 1
    SLOTS = K + 1
    BIG = 1e30
    NO_NODE = 1000000
    CT = 7
    CHUNKS = NT // CT
    ACT_TILES = 4
    XB = 4
    BLOCKS = -(-NT // XB)
    assert NS % P == 0 and NT % CT == 0 and K * HEADS == P and TAIL_E and TAIL_N
    assert NG % RING == 0 and BLOCKS * XB <= RING * K

    def dram(name, shape, dt):
        return nc.dram_tensor(name, shape, dt, kind="Internal").ap()

    edge_rows = dram("edge_rows", [ET, 3 * P], i32)
    hi_rows = dram("hi_rows", [NT * P, WX], fp32)
    x1_rows = dram("x1_rows", [NT * P, C], fp32)
    locals_flat = dram("locals_flat", [1 + NS * P], fp32)
    starts_flat = dram("starts_flat", [NS * P + P], fp32)
    through_flat = dram("through_flat", [2, NS], fp32)

    ctx = ExitStack()
    with ctx:
        def sb(name, shape, dt=fp32):
            return ctx.enter_context(nc.sbuf_tensor(name, shape, dt))

        def ps(name, shape=(P, 512), dt=fp32):
            return ctx.enter_context(nc.psum_tensor(name, list(shape), dt))

        def sem(name):
            return ctx.enter_context(nc.semaphore(name))

        def sems(names):
            return [sem(n) for n in names.split()]

        neg_iota = sb("neg_iota", [P, P])
        tile_no = sb("tile_no", [P, SM])
        step_no = sb("step_no", [P, SM])
        ident = sb("ident", [P, P])
        ones_bf = sb("ones_bf", [P, P], bf16)
        a_relu = sb("a_relu", [P, C])
        pads = sb("pads", [1, 3, P], i32)
        eps_col = sb("eps_col", [P, 1])
        one_col = sb("one_col", [P, 1])
        last_dst = sb("last_dst", [P, SM], i32)
        last_tile = sb("last_tile", [P, SM], i32)
        ends_at = sb("ends_at", [P, SM])
        node_tile_row = sb("node_tile_row", [1, NS + K], i16)
        edge_tile_col = sb("edge_tile_col", [P, SM], i32)
        first_node = sb("first_node", [P, SM])
        src_idx = sb("src_idx", [P, NS + 3 * K], i16)
        neg_local = sb("neg_local", [P, NS + K], bf16)
        weight = sb("weight", [P, NS])
        x_sb = sb("x_sb", [P, NT, C])
        hj = sb("hj", [P, NA, WX])
        acc = sb("acc", [P, NA, 2, WX])
        idx_g = sb("idx_g", [P, RING, K], i32)
        rows = sb("rows", [P, RING * K, WX])
        S = sb("S", [P, RING * K, P])
        logits = sb("logits", [P, RING, HEADS, K])
        neg_local_g = sb("neg_local_g", [P, 2, K])
        weight_g = sb("weight_g", [P, 2, K])
        starts = sb("starts", [P, 2, P + 1])
        through = sb("through", [1, 2, 2, HEADS, SLOTS])
        rescale = sb("rescale", [P, 2, HEADS])
        ST = sb("ST", [P, 2, B * P])
        weighted = sb("weighted", [P, B * P])
        scan_a = sb("scan_a", [P, P])
        scan_b = sb("scan_b", [P, P])
        last_max = sb("last_max", [1, HEADS, SLOTS])
        first_max = sb("first_max", [1, HEADS, SLOTS])
        up = sb("up", [1, HEADS, SLOTS])
        down = sb("down", [1, HEADS, SLOTS])
        updown = sb("updown", [1, 2, P])
        shift = sb("shift", [1, 2, HEADS])
        below = sb("below", [P, P])
        stats = sb("stats", [P, CT, 6])
        mv = sb("mv", [P, 2, CT, 2])
        rstd = sb("rstd", [P, 2, 3, CT])
        small = sb("small", [P, 4, SM])
        w12 = logits[:, :, :, :].rearrange("p r h k -> p (r h k)")[:, 0:2 * WX].rearrange("p (a w) -> p a w", a=2)
        a_rep = scan_a
        tab_f = weighted[:, :].rearrange("p (a q e) -> p a q e", a=2, q=2)

        flat_S = S[:, :, :].rearrange("p k n -> p (k n)")
        passed = flat_S[:, 0:NS].bitcast(bf16).rearrange("p (a s) -> p a s", a=2)
        iota = flat_S[:, NS:2 * NS]
        local_s = flat_S[:, 0:SM * P].rearrange("p (m e) -> p m e", m=SM)
        prev_s = flat_S[:, SM * P:2 * SM * P].rearrange("p (m e) -> p m e", m=SM)
        TR = 8
        tables = flat_S[:, 2 * NS:2 * NS + TR * 3 * P].bitcast(i32).rearrange("p (m q e) -> p m q e", m=TR, q=3)
        edge_tile_row = flat_S[0:1, 2 * NS + TR * 3 * P:3 * NS + TR * 3 * P]
        work = rows[:, :, :].rearrange("p k w -> p (k w)")[:, 0:2 * CT * C].rearrange("p (b t c) -> p b t c", b=2, t=CT)
        fin = rows[:, :, :].rearrange("p k w -> p (k w)")[:, 2 * CT * C:2 * CT * C + 2 * 5 * CT * HEADS].rearrange(
            "p (b i t h) -> p b i t h", b=2, i=5, t=CT)

        psU = [ps("psU0"), ps("psU1")]
        psL = ps("psL")
        psT = ps("psT")
        psP = [ps("psP0"), ps("psP1")]
        psA = ps("psA")
        psB = ps("psB")

        consts, memsets, fills, fills2 = sems("consts memsets fills fills2")
        w_in, x_in, last_in, rows_made = sems("w_in x_in last_in rows_made")
        pre, w_ready = sems("pre w_ready")
        passed_ready, passed_used, tiles_row, col_ps, col_ready = sems(
            "passed_ready passed_used tiles_row col_ps col_ready")
        xT_ps, xT_sb, h_ps = sems("xT_ps xT_sb h_ps")
        h_sb = sems("h_sb0 h_sb1")
        hi_out = sem("hi_out")
        table_in = [sem(f"table_in{m}") for m in range(TR)]
        tab_ready, tab_ps, tab_out, local_out = sems("tab_ready tab_ps tab_out local_out")
        locals_out, prev_in, starts_out, next_in, through_out = sems(
            "locals_out prev_in starts_out next_in through_out")
        starts_made, through_made, node_tiles_ready = sems("starts_made through_made node_tiles_ready")
        idx_ready, neg_ready = sems("idx_ready neg_ready")
        rows_in = [[sem(f"rows_in{p}{j}") for j in range(J)] for p in range(RING)]
        flags_in = [sem("flags_in0"), sem("flags_in1")]
        square_done, S_ready, ST_ps, ST_sb, U_ready, relu_done, reduced, logits_ready = sems(
            "square_done S_ready ST_ps ST_sb U_ready relu_done reduced logits_ready")
        logitsT, scan1, scan2, rows_ps, rows_sb, scan_up, updown_sb, updown_ps, scan3, scan4, maxT = sems(
            "logitsT scan1 scan2 rows_ps rows_sb scan_up updown_sb updown_ps scan3 scan4 maxT")
        shift1, shift2, below_ready, weights_ready, rescale_ps, rescale_log, rescale_sb, rescaled = sems(
            "shift1 shift2 below_ready weights_ready rescale_ps rescale_log rescale_sb rescaled")
        msg_ready, sums_ps, added = sems("msg_ready sums_ps added")
        idx1_ready, local1_ready, S1_ready, sums1_ps, added1 = sems(
            "idx1_ready local1_ready S1_ready sums1_ps added1")
        rows1_in = [[sem(f"rows1_in{p}{j}") for j in range(J)] for p in range(RING)]
        fin_merged, fin_v, fin_stats, fin_var, fin_std, fin_rs, fin_act, fin_dve = (
            [sem(f"{n}{rnd}") for rnd in range(2)] for n in
            "fin_merged fin_v fin_stats fin_var fin_std fin_rs fin_act fin_dve".split())
        x1_out, out_done, acc1_zero, acc1_odd_zero = sems("x1_out out_done acc1_zero acc1_odd_zero")
        passed_by = {e: sem(f"passed_by_{e}") for e in ("pe", "pool")}

        block = ctx.enter_context(nc.Block())

        def number(G):
            return G[0] * RING + G[1]

        def half(G):
            return G[0] * (RING // 2) + G[1] // 2

        def lap(G):
            return G[0] + G[1] // RING

        def slot(G):
            return G[1] % RING * K

        def parity(G):
            return G[1] % 2

        def near(G, n):
            return G[0], G[1] + n

        def early(G, n):
            return isinstance(G[0], int) and number(G) < n

        def groups(engine, one):
            for g in range(RING):
                one((0, g))
            with engine.Fori(0, NG // RING - 1) as it:
                base = engine.snap(it + 1)
                for step in range(RING):
                    one((base, step))

        def last_group(n=0):
            return 0, NG - 1 + n

        def block_tiles(m):
            return range(m * XB, min(m * XB + XB, NT))

        def merge(engine, c, width, done):
            at = acc[:, c * CT:(c + 1) * CT, :, 0:width]
            engine.tensor_tensor(at[:, :, 0, :], at[:, :, 0, :], at[:, :, 1, :], ALU.add).then_inc(done, 1)

        @block.sync
        def _(sp):
            sp.wait_ge(memsets, 3)
            tiles = dst[0:FULL_E * P].rearrange("(i e) -> i e", e=P)[:, P - 1:P]
            whole = FULL_E // SM
            with nc.allow_non_contiguous_dma(reason="one element of each edge tile"):
                sp.dma_start(last_dst[0:whole, :],
                             tiles[0:whole * SM, :].rearrange("(p c) o -> p (c o)", c=SM)).then_inc(last_in, 16)
                sp.dma_start(last_dst[whole:whole + 1, 0:FULL_E - whole * SM],
                             tiles[whole * SM:FULL_E, :].rearrange("(p c) o -> p (c o)", p=1)).then_inc(last_in, 16)
            sp.dma_start(w12[:, 0, 0:C], w1).then_inc(w_in, 16)
            sp.dma_start(w12[:, 1, 0:C], w2).then_inc(w_in, 16)
            sp.dma_start(a_rep[:, :], a[0, :].partition_broadcast(P)).then_inc(w_in, 16)
            sp.wait_ge(fills, 1)
            sp.dma_start(x_sb[:, 0:FULL_N, :], x[0:FULL_N * P, :].rearrange("(t p) c -> p t c", p=P)).then_inc(x_in, 16)
            sp.dma_start(x_sb[0:TAIL_N, FULL_N, :], x[FULL_N * P:N, :]).then_inc(x_in, 16)
            even = FULL_E // 16 * 16
            for q, v in enumerate((src, dst, edge_weight.bitcast(i32))):
                full = v[0:FULL_E * P].rearrange("(i e) -> i e", e=P)
                sp.dma_start(edge_rows[0:even, q * P:q * P + P], full[0:even, :]).then_inc(rows_made, 16)
                sp.dma_start(edge_rows[even:FULL_E, q * P:q * P + P], full[even:FULL_E, :]).then_inc(rows_made, 16)
                sp.dma_start(edge_rows[FULL_E:ET, q * P:q * P + TAIL_E],
                             v[FULL_E * P:E].rearrange("(o e) -> o e", o=1)).then_inc(rows_made, 16)
                sp.dma_start(edge_rows[FULL_E:ET, q * P + TAIL_E:q * P + P], pads[:, q, TAIL_E:P]).then_inc(rows_made, 16)
            for m in range(BLOCKS):
                ts = block_tiles(m)
                sp.wait_ge(h_sb[0], 2 * (ts[-1] // 2 + 1))
                sp.wait_ge(h_sb[1], 2 * ((ts[-1] + 1) // 2))
                s0 = m * XB
                sp.dma_start(hi_rows[ts[0] * P:(ts[-1] + 1) * P, :].rearrange("(t p) c -> p t c", p=P),
                             rows[:, s0:s0 + len(ts), :]).then_inc(hi_out, 16)
            flat = locals_flat[1:1 + NS * P].rearrange("(m p e) -> p m e", p=P, e=P)
            sp.dma_start(locals_flat[0:1].rearrange("(o e) -> o e", o=1), eps_col[0:1, 0:1]).then_inc(locals_out, 16)
            sp.wait_ge(tab_ready, 2 * SM)
            sp.dma_start(flat, local_s).then_inc(locals_out, 16)
            sp.wait_ge(locals_out, 32)
            sp.dma_start(prev_s, locals_flat[0:NS * P].rearrange("(m p e) -> p m e", p=P, e=P)).then_inc(prev_in, 16)
            sp.wait_ge(starts_made, 1)
            sp.dma_start(starts_flat[0:NS * P].rearrange("(m p e) -> p m e", p=P, e=P), prev_s).then_inc(starts_out, 16)
            sp.dma_start(starts_flat[NS * P:NS * P + 1].rearrange("(o e) -> o e", o=1), small[0:1, 3, 0:1]).then_inc(starts_out, 16)
            sp.wait_ge(starts_out, 32)
            with nc.allow_non_contiguous_dma(reason="one element of each step"):
                sp.dma_start(small[:, 0, :].rearrange("p (m o) -> p m o", o=1),
                             starts_flat[P:P + NS * P].rearrange("(m p e) -> p m e", p=P, e=P)[:, :, 0:1]).then_inc(next_in, 16)
                sp.wait_ge(through_made, 2)
                sp.dma_start(through_flat[0, :].rearrange("(m p) -> p m", p=P), small[:, 1, :]).then_inc(through_out, 16)
                sp.dma_start(through_flat[1, :].rearrange("(m p) -> p m", p=P), small[:, 2, :]).then_inc(through_out, 16)
            sp.wait_ge(through_out, 32)

            def flags(G):
                if not early(G, 2):
                    sp.wait_ge(scan4, number(G) - 1)
                part = starts_flat[ds(number(G) * (K * P), K * P + P)]
                for h in range(HEADS):
                    sp.dma_start(starts[h * K:h * K + K, parity(G), 0:P], part[0:K * P].rearrange("(k e) -> k e", e=P)) \
                        .then_inc(flags_in[parity(G)], 16)
                    sp.dma_start(starts[h * K:h * K + K, parity(G), P:P + 1],
                                 part[P:K * P + P].rearrange("(k e) -> k e", e=P)[:, 0:1]).then_inc(flags_in[parity(G)], 16)
                for d in range(2):
                    sp.dma_start(through[0:1, parity(G), d, :, 1 - d:1 - d + K],
                                 through_flat[d:d + 1, ds(number(G) * K, K)].rearrange("o (b k) -> o b k", b=1)
                                 .to_broadcast([1, HEADS, K])).then_inc(flags_in[parity(G)], 16)

            with nc.allow_non_contiguous_dma(reason="the next tile's first element"):
                groups(sp, flags)

            for rnd, (table, done) in enumerate(((x1_rows, x1_out), (out, out_done))):
                for c in range(CHUNKS):
                    sp.wait_ge(fin_act[rnd], (c + 1) * ACT_TILES)
                    sp.wait_ge(fin_dve[rnd], (c + 1) * (CT - ACT_TILES))
                    t0, t1 = c * CT, (c + 1) * CT
                    if rnd == 1 and c == CHUNKS - 1:
                        t1 = FULL_N
                    sp.dma_start(table[t0 * P:t1 * P, :].rearrange("(t p) c -> p t c", p=P), x_sb[:, t0:t1, :]).then_inc(done, 16)
            sp.dma_start(out[FULL_N * P:N, :], x_sb[0:TAIL_N, FULL_N, :]).then_inc(out_done, 16)
            sp.wait_ge(out_done, 16 * (CHUNKS + 1))

        @block.gpsimd
        def _(pool):
            pool.memset(last_dst[:, :], NO_NODE).then_inc(memsets, 1)
            pool.memset(pads[:, :, :], 0).then_inc(memsets, 1)
            pool.wait_ge(memsets, 2)
            pool.memset(pads[:, 1, :], NO_NODE).then_inc(memsets, 1)
            pool.iota(tile_no[:, :], [[1, SM]], base=0, channel_multiplier=SM,
                      allow_small_or_imprecise_dtypes=True).then_inc(consts, 1)
            pool.memset(ones_bf[:, :], 1.0).then_inc(consts, 1)
            pool.memset(ident[:, :], 0.0).then_inc(consts, 1)
            pool.wait_ge(consts, 3)
            pool.affine_select(out=ident[:, :], in_=ident[:, :], compare_op=ALU.not_equal, fill=1.0,
                               base=0, pattern=[[-1, P]], channel_multiplier=1).then_inc(consts, 1)
            pool.iota(iota, [[1, NS]], base=0, channel_multiplier=0,
                      allow_small_or_imprecise_dtypes=True).then_inc(consts, 1)
            pool.iota(step_no[:, :], [[P, SM]], base=0, channel_multiplier=1,
                      allow_small_or_imprecise_dtypes=True).then_inc(consts, 1)
            pool.iota(neg_iota[:, :], [[-1, P]], base=0, channel_multiplier=0,
                      allow_small_or_imprecise_dtypes=True).then_inc(consts, 1)
            pool.memset(acc[:, :, :, :], 0.0).then_inc(fills2, 1)
            pool.wait_ge(rows_made, 16 * 12)
            pool.wait_ge(col_ready, 1)
            for m in range(SM):
                if m >= TR:
                    pool.wait_ge(tab_ready, 2 * (m - TR + 1))
                    pool.wait_ge(tab_ps, m - TR + 1)
                pool.indirect_dma_start(tables[:, m % TR, :, :].rearrange("p q e -> p (q e)"), None, edge_rows,
                                        bass.IndirectOffsetOnAxis(ap=edge_tile_col[:, m:m + 1], axis=0)) \
                    .then_inc(table_in[m % TR], 16)

            pool.wait_ge(hi_out, 16 * BLOCKS)
            for rnd, (table, width, arrived, ready, used) in enumerate((
                    (hi_rows, WX, rows_in, idx_ready, sums_ps), (x1_rows, C, rows1_in, idx1_ready, sums1_ps))):
                if rnd == 1:
                    for c in range(CHUNKS):
                        pool.wait_ge(added, NS)
                        merge(pool, c, WX, fin_merged[0])
                    pool.wait_ge(fin_merged[0], CHUNKS)
                    pool.memset(acc[:, :, 1, :], 0.0).then_inc(acc1_odd_zero, 1)
                    pool.wait_ge(x1_out, 16 * CHUNKS)

                def gather(G):
                    pool.wait_ge(ready, number(G) + 1)
                    for j in range(J):
                        if not early(G, RING):
                            pool.wait_ge(used, number(G) * (2 * J) + 2 * (j + 1 - RING * J))
                            pool.sem_inc(passed_by["pool"], 1)
                        for k in range(j * B, j * B + B):
                            pool.indirect_dma_start(rows[:, slot(G) + k, 0:width], None, table,
                                                    bass.IndirectOffsetOnAxis(ap=idx_g[:, slot(G) // K, k:k + 1], axis=0)) \
                                .then_inc(arrived[slot(G) // K][j], 16)

                groups(pool, gather)
            for c in range(CHUNKS):
                pool.wait_ge(added1, NS)
                merge(pool, c, W1, fin_merged[1])

        @block.tensor
        def _(pe):
            quarters = [psU[0], psU[1], psL, psT]
            pe.wait_ge(consts, 7)
            pe.wait_ge(x_in, 32)

            def turn(m):
                if m >= 2:
                    pe.wait_ge(xT_sb, m - 1)
                for i, t in enumerate(block_tiles(m)):
                    tr = pe.transpose((psA, psB)[m % 2][:, i * P:i * P + P], x_sb[:, t, :], ident[:, :])
                tr.then_inc(xT_ps, 1)

            turn(0)
            for m in range(max(BLOCKS, SM)):
                if m + 1 < BLOCKS:
                    turn(m + 1)
                if m < SM:
                    pe.wait_ge(passed_ready, m + 1)
                    for q in range(4):
                        mm = pe.matmul(quarters[q][:, 0:QW], ones_bf[:, :], passed[:, m % 2, q * QW:(q + 1) * QW],
                                       start=(m == 0), stop=(m == SM - 1))
                    mm.then_inc(passed_used, 1)
                if m < BLOCKS:
                    pe.wait_ge(xT_sb, m + 1)
                    pe.wait_ge(w_ready, 2)
                    for i, t in enumerate(block_tiles(m)):
                        if t >= 2:
                            pe.wait_ge(h_sb[t % 2], 2 * (t // 2))
                        pe.matmul(psP[t % 2][:, 0:2 * WX], ST[:, m % 2, i * P:i * P + P],
                                  w12[:, :, :].rearrange("p a w -> p (a w)"), start=True, stop=True).then_inc(h_ps, 1)
                if m == SM - 1:
                    pe.wait_ge(tiles_row, 4)
                    pe.wait_ge(xT_sb, BLOCKS)
                    for c in range(SM):
                        tr = pe.transpose(psA[:, c:c + 1], edge_tile_row[0:1, c * P:c * P + P], ident[0:1, 0:1])
                    tr.then_inc(col_ps, 1)
            for m in range(SM):
                bank = (psT, psL)[m % 2]
                pe.wait_ge(tab_ready, 2 * m + 2)
                pe.wait_ge(table_in[m % TR], 16 * (m // TR + 1))
                if m >= 2:
                    pe.wait_ge(tab_out, m - 1)
                    pe.wait_ge(local_out, m - 1)
                pe.transpose(bank[:, 0:P], tab_f[:, m % 2, 0, :], ident[:, :])
                pe.transpose(bank[:, P:2 * P], local_s[:, m, :], ident[:, :])
                pe.transpose(bank[:, 2 * P:3 * P], tables[:, m % TR, 2, :].bitcast(fp32), ident[:, :]).then_inc(tab_ps, 1)

            def turn_S(G, j):
                b = number(G) * J + j
                pe.wait_ge(S_ready, b + 1)
                if not (early(G, 1) and j == 0):
                    pe.wait_ge(ST_sb, b)
                for k in range(B):
                    tr = pe.transpose(psT[:, k * P:k * P + P], S[:, slot(G) + j * B + k, :], ident[:, :])
                tr.then_inc(ST_ps, 1)

            tile_of = [0] * K

            def node_tiles(G):
                _, values = nc.values_load_multi_w_load_instructions(
                    node_tile_row[0:1, ds(number(G) * K, K)], [mybir.EngineType.PE], min_val=0, max_val=NA - 1,
                    skip_runtime_bounds_check_because="a step's node tile is at most NT")
                tile_of[:] = values

            def spread(G, j):
                b = number(G) * J + j
                s0 = slot(G) + j * B
                pe.wait_ge(rows_in[slot(G) // K][j], (lap(G) + 1) * (16 * B))
                if not (early(G, 1) and j < 2):
                    pe.wait_ge(relu_done, b - 1)
                if j == 0 and not early(G, 1):
                    pe.wait_ge(logits_ready, number(G))
                U = psU[j % 2]
                linear = psL[:, 0:P].rearrange("p (h k) -> p k h", k=K)
                pe.matmul(U[:, :], ident[:, :], rows[:, s0:s0 + B, 0:C], start=True, stop=True, skip_group_check=True)
                pe.matmul(linear[:, j * B:j * B + B, :], ident[:, :], rows[:, s0:s0 + B, C:WX],
                          start=True, stop=True, skip_group_check=True)
                pe.wait_ge(ST_sb, b + 1)
                for k in range(B):
                    left, tile = ST[:, j % 2, k * P:k * P + P], ds(tile_of[j * B + k], 1)
                    pe.matmul(U[:, k * P:k * P + P], left, hj[:, tile, 0:C], start=False, stop=True, skip_group_check=True)
                    mm = pe.matmul(linear[:, j * B + k, :], left, hj[:, tile, C:WX], start=False, stop=True,
                                   skip_group_check=True)
                mm.then_inc(U_ready, 1)

            def turn_logits(Q):
                q = number(Q)
                pe.wait_ge(logits_ready, q + 1)
                if not early(Q, 1):
                    pe.wait_ge(scan4, q)
                if not early(Q, 2):
                    pe.wait_ge(below_ready, q - 1)
                    pe.sem_inc(passed_by["pe"], 1)
                pe.transpose(psA[:, 0:P], logits[:, slot(Q) // K, :, :].rearrange("p h k -> p (h k)"), ident[:, :]).then_inc(logitsT, 1)

            def turn_ends(Q):
                q = number(Q)
                pe.wait_ge(scan2, q + 1)
                if not early(Q, 2):
                    pe.wait_ge(rescale_log, q - 1)
                pe.transpose(psB[0:1, 0:P], scan_b[:, P - 1:P], ident[:, :])
                pe.transpose(psB[0:1, P:2 * P], scan_b[:, 0:1], ident[:, :]).then_inc(rows_ps, 1)

            def turn_updown(Q):
                pe.wait_ge(updown_sb, number(Q) * 2 + 2)
                pe.sem_inc(passed_by["pe"], 1)
                pe.transpose(psB[:, 256:257], updown[0:1, 0, :], ident[0:1, 0:1])
                pe.transpose(psB[:, 257:258], updown[0:1, 1, :], ident[0:1, 0:1]).then_inc(updown_ps, 1)

            def turn_max(Q):
                pe.wait_ge(scan4, number(Q) + 1)
                if not early(Q, 1):
                    pe.wait_ge(below_ready, number(Q))
                    pe.sem_inc(passed_by["pe"], 1)
                pe.transpose(psA[:, P:2 * P], scan_b[:, :], ident[:, :]).then_inc(maxT, 1)

            def spread_shift(Q, more):
                if more:
                    pe.wait_ge(rows_sb, number(Q) * 3 + 6)
                    pe.sem_inc(passed_by["pe"], 1)
                pe.wait_ge(shift2, number(Q) + 1)
                pe.matmul(psB[:, 264:264 + HEADS], S[0:1, slot(Q), :], shift[0:1, 1, :], start=True, stop=True) \
                    .then_inc(rescale_ps, 1)

            def sums(Q, j):
                pe.wait_ge(msg_ready, number(Q) * J + (j + 1))
                for i in range(2):
                    n = (number(Q) * J + j) * 2 + i
                    if not (early(Q, 1) and j == 0):
                        pe.wait_ge(added, n * 2 - 2)
                    for e in range(2):
                        k = j * B + i * 2 + e
                        mm = pe.matmul(psP[i][:, e * 256:e * 256 + WX], S[:, slot(Q) + k, :], rows[:, slot(Q) + k, :],
                                       start=True, stop=True)
                    mm.then_inc(sums_ps, 1)

            def weave(G, spreads=True, chain=True, middle=True, summing=True):
                H, Q, O, L = (near(G, n) for n in (1, -1, -2, -3))
                for j in range(J):
                    if spreads:
                        if j == 0:
                            node_tiles(G)
                        turn_S(G if j + 1 < J else H, (j + 1) % J)
                        spread(G, j)
                    if j + 1 < J and summing:
                        sums(L, j + 1)
                    if j + 1 == J and middle:
                        sums(O, 0)
                    if j == 0 and chain:
                        turn_logits(Q)
                    if j == 0 and middle:
                        turn_max(O)
                    if j == 1 and chain:
                        turn_ends(Q)
                    if j == 2 and middle:
                        spread_shift(O, chain)
                    if j == 2 and chain:
                        turn_updown(Q)

            pe.wait_ge(node_tiles_ready, 2)
            turn_S((0, 0), 0)
            groups(pe, lambda G: weave(G, chain=not early(G, 1), middle=not early(G, 2), summing=not early(G, 3)))
            weave(last_group(1), spreads=False)
            weave(last_group(2), spreads=False, chain=False)
            weave(last_group(3), spreads=False, chain=False, middle=False)

            def sums1(G):
                for j in range(J):
                    pe.wait_ge(rows1_in[slot(G) // K][j], (lap(G) + 1) * (16 * B))
                    pe.wait_ge(S1_ready, number(G) * J + (j + 1))
                    for i in range(2):
                        n = (number(G) * J + j) * 2 + i
                        if not (early(G, 1) and j == 0):
                            pe.wait_ge(added1, n * 2 - 2)
                        for e in range(2):
                            k = slot(G) + j * B + i * 2 + e
                            mm = pe.matmul(psP[i][:, e * 256:e * 256 + W1], S[:, k, :], rows[:, k, 0:W1],
                                           start=True, stop=True)
                        mm.then_inc(sums1_ps, 1)

            pe.wait_ge(acc1_zero, 2)
            groups(pe, sums1)

        @block.scalar
        def _(act):
            for m in range(BLOCKS):
                ts = block_tiles(m)
                act.wait_ge(xT_ps, m + 1)
                if m >= 2:
                    act.wait_ge(h_ps, block_tiles(m - 2)[-1] + 1)
                act.activation(ST[:, m % 2, 0:len(ts) * P], (psA, psB)[m % 2][:, 0:len(ts) * P], ACT.Copy).then_inc(xT_sb, 1)
                for i, t in enumerate(ts):
                    if t % 2 == 0:
                        act.wait_ge(h_ps, t + 1)
                        act.activation(rows[:, m * XB + i, :], psP[0][:, 0:WX], ACT.Copy).then_inc(h_sb[0], 1)
                        act.activation(hj[:, t, :], psP[0][:, WX:2 * WX], ACT.Copy).then_inc(h_sb[0], 1)

            def onehot(G, j):
                g = number(G)
                act.wait_ge(neg_ready, g + 1)
                if not early(G, RING):
                    act.wait_ge(sums_ps, g * (2 * J) + (2 * (j + 1) - 2 * RING * J))
                s0 = slot(G) + j * B
                for k in range(B):
                    op = act.activation(S[:, s0 + k, :], neg_iota[:, :], ACT.Square, scale=-1.0,
                                        bias=neg_local_g[:, parity(G), j * B + k:j * B + k + 1])
                op.then_inc(square_done, 1)
                act.wait_ge(square_done, g * J + (j + 1))
                act.activation(S[:, s0:s0 + B, :], S[:, s0:s0 + B, :], ACT.Relu, scale=-1.0, bias=one_col[:, :]).then_inc(S_ready, 1)

            def copy_ST(G, j):
                b = number(G) * J + j
                act.wait_ge(ST_ps, b + 1)
                if not (early(G, 1) and j < 2):
                    act.wait_ge(U_ready, b - 1)
                act.activation(ST[:, j % 2, :], psT[:, :], ACT.Copy).then_inc(ST_sb, 1)

            def exps(Q):
                q = number(Q)
                act.wait_ge(below_ready, q + 1)
                act.activation(rows[:, slot(Q):slot(Q) + K, C:WX].rearrange("p k h -> p h k"),
                               below[:, :].rearrange("p (h k) -> p h k", k=K), ACT.Exp).then_inc(weights_ready, 1)

            def exp_shift(Q):
                act.wait_ge(rescale_log, number(Q) + 1)
                act.activation(rescale[:, parity(Q), :], rescale[:, parity(Q), :], ACT.Exp).then_inc(rescale_sb, 1)

            def weave(G):
                H, O = near(G, 1), near(G, -2)
                copy_ST(G, 1)
                onehot(H, 0)
                copy_ST(G, 2)
                if not early(G, 2):
                    exps(O)
                onehot(H, 1)
                copy_ST(G, 3)
                onehot(H, 2)
                copy_ST(H, 0)
                if not early(G, 2):
                    exp_shift(O)
                onehot(H, 3)

            act.wait_ge(through_made, 2)
            act.wait_ge(starts_out, 32)
            for j in range(J):
                onehot((0, 0), j)
                if j == 0:
                    copy_ST((0, 0), 0)
            groups(act, weave)
            for n in (-1, 0):
                exps(last_group(n))
                exp_shift(last_group(n))

            for rnd in range(2):
                for c in range(CHUNKS + 1):
                    if c < CHUNKS:
                        act.wait_ge(fin_var[rnd], c + 1)
                        act.activation(rstd[:, c % 2, 0, :], mv[:, c % 2, :, 1], ACT.Sqrt, bias=eps_col[:, :]).then_inc(fin_std[rnd], 1)
                    if c >= 1:
                        act.wait_ge(fin_rs[rnd], c)
                        for i in range(ACT_TILES):
                            xt = x_sb[:, (c - 1) * CT + i, :]
                            act.activation(xt, xt, ACT.Identity, bias=rstd[:, (c - 1) % 2, 2, i:i + 1],
                                           scale=rstd[:, (c - 1) % 2, 1, i:i + 1]).then_inc(fin_act[rnd], 1)

        @block.vector
        def _(dve):
            dve.memset(x_sb[:, FULL_N:NT, :], 0.0).then_inc(fills, 1)
            dve.memset(eps_col[:, :], EPS_NORM).then_inc(fills, 1)
            dve.memset(one_col[:, :], 1.0).then_inc(fills, 1)
            dve.memset(small[:, 3, :], -BIG).then_inc(fills, 1)
            dve.memset(up[:, :, :], -BIG).then_inc(fills, 1)
            dve.memset(first_max[:, :, :], -BIG).then_inc(fills, 1)
            dve.wait_ge(last_in, 32)
            dve.wait_ge(consts, 7)
            dve.tensor_scalar(last_tile[:, :], last_dst[:, :], P.bit_length() - 1, None, ALU.logical_shift_right).then_inc(pre, 1)
            dve.wait_ge(pre, 1)
            dve.tensor_tensor(ends_at[:, :], last_tile[:, :], tile_no[:, :], ALU.add).then_inc(pre, 1)
            dve.wait_ge(pre, 2)

            def compare(c):
                if c >= 2:
                    dve.wait_ge(passed_used, c - 1)
                dve.tensor_scalar(passed[:, c % 2, :], iota, ends_at[:, c:c + 1], None, ALU.is_gt).then_inc(passed_ready, 1)

            compare(0)
            compare(1)
            dve.wait_ge(w_in, 48)
            for i in range(2):
                dve.tensor_tensor(weighted[:, i * C:i * C + C], w12[:, i, 0:C], a_rep[:, :], ALU.mult).then_inc(pre, 1)
            dve.tensor_scalar(a_relu[:, :], a_rep[:, :], 1.0 - SLOPE, None, ALU.mult).then_inc(pre, 1)
            dve.wait_ge(pre, 5)
            for i in range(2):
                dve.tensor_reduce(w12[:, i, C:WX], weighted[:, i * C:i * C + C].rearrange("p (h c) -> p h c", h=HEADS),
                                  AX.X, ALU.add).then_inc(pre, 1)
            dve.wait_ge(pre, 7)
            for i in range(2):
                dve.tensor_scalar(w12[:, i, C:WX], w12[:, i, C:WX], SLOPE, None, ALU.mult).then_inc(w_ready, 1)
            for m in range(max(BLOCKS, SM)):
                if m + 2 < SM:
                    compare(m + 2)
                if m == SM - 1:
                    dve.wait_ge(passed_used, SM)
                    for q, bank in enumerate((psU[0], psU[1], psL, psT)):
                        dve.tensor_copy(edge_tile_row[:, q * QW:(q + 1) * QW], bank[0:1, 0:QW]).then_inc(tiles_row, 1)
                if m < BLOCKS:
                    for i, t in enumerate(block_tiles(m)):
                        if t % 2:
                            dve.wait_ge(h_ps, t + 1)
                            dve.tensor_copy(rows[:, m * XB + i, :], psP[1][:, 0:WX]).then_inc(h_sb[1], 1)
                            dve.tensor_copy(hj[:, t, :], psP[1][:, WX:2 * WX]).then_inc(h_sb[1], 1)
            dve.wait_ge(tiles_row, 4)
            dve.tensor_tensor(node_tile_row[:, 0:NS], iota[0:1, :], edge_tile_row, ALU.subtract).then_inc(pre, 1)
            dve.wait_ge(col_ps, 1)
            dve.tensor_copy(edge_tile_col[:, :], psA[:, 0:SM]).then_inc(col_ready, 1)
            dve.tensor_tensor(first_node[:, :], step_no[:, :], psA[:, 0:SM], ALU.subtract).then_inc(pre, 1)
            dve.memset(node_tile_row[:, NS:NS + K], 0).then_inc(node_tiles_ready, 1)
            dve.wait_ge(pre, 8)
            dve.tensor_scalar(node_tile_row[:, 0:NS], node_tile_row[:, 0:NS], float(NT), None, ALU.min).then_inc(node_tiles_ready, 1)
            dve.wait_ge(pre, 9)
            dve.tensor_scalar(first_node[:, :], first_node[:, :], float(P), None, ALU.mult).then_inc(pre, 1)
            dve.memset(hj[:, NT:NA, :], 0.0).then_inc(fills, 1)
            dve.memset(src_idx[:, NS:NS + 3 * K], 0).then_inc(fills, 1)
            dve.memset(neg_local[:, NS:NS + K], 0.0).then_inc(fills, 1)
            dve.memset(through[:, :, :, :, :], -BIG).then_inc(fills, 1)
            dve.wait_ge(pre, 10)
            def spread_table(m):
                if m >= 2:
                    dve.wait_ge(tab_ps, m - 1)
                dve.wait_ge(table_in[m % TR], 16 * (m // TR + 1))
                dve.tensor_copy(tab_f[:, m % 2, 0, :], tables[:, m % TR, 0, :]).then_inc(tab_ready, 1)
                dve.tensor_scalar(local_s[:, m, :], tables[:, m % TR, 1, :], first_node[:, m:m + 1], None,
                                  ALU.subtract).then_inc(tab_ready, 1)

            spread_table(0)
            for m in range(SM):
                if m + 1 < SM:
                    spread_table(m + 1)
                bank = (psT, psL)[m % 2]
                at = slice(m * P, m * P + P)
                dve.wait_ge(tab_ps, m + 1)
                dve.tensor_copy(src_idx[:, at], bank[:, 0:P])
                dve.tensor_copy(weight[:, at], bank[:, 2 * P:3 * P]).then_inc(tab_out, 1)
                dve.tensor_scalar(neg_local[:, at], bank[:, P:2 * P], -1.0, None, ALU.mult).then_inc(local_out, 1)

            def next_idx(G, ready):
                dve.tensor_copy(idx_g[:, slot(G) // K, :], src_idx[:, ds(number(G) * K, K)]).then_inc(ready, 1)

            def next_local(G):
                dve.tensor_copy(neg_local_g[:, parity(G), :], neg_local[:, ds(number(G) * K, K)]).then_inc(neg_ready, 1)

            dve.wait_ge(tab_out, SM)
            dve.wait_ge(local_out, SM)
            dve.wait_ge(fills, 10)
            for g in range(3):
                next_idx((0, g), idx_ready)
            next_local((0, 0))
            dve.wait_ge(prev_in, 16)
            dve.tensor_tensor(prev_s, local_s, prev_s, ALU.not_equal).then_inc(pre, 1)
            dve.wait_ge(pre, 11)
            dve.tensor_scalar(prev_s, prev_s, -BIG, None, ALU.mult).then_inc(starts_made, 1)
            dve.wait_ge(starts_made, 1)
            dve.tensor_reduce(first_node[:, :], prev_s[:, :, 1:P], AX.X, ALU.min).then_inc(pre, 1)
            dve.wait_ge(pre, 12)
            dve.tensor_tensor(small[:, 1, :], first_node[:, :], prev_s[:, :, 0], ALU.add).then_inc(through_made, 1)
            dve.wait_ge(next_in, 16)
            dve.tensor_tensor(small[:, 2, :], first_node[:, :], small[:, 0, :], ALU.add).then_inc(through_made, 1)

            def relu(G, j):
                b = number(G) * J + j
                if not (early(G, 1) and j == 0):
                    dve.wait_ge(reduced, b)
                dve.wait_ge(U_ready, b + 1)
                dve.scalar_tensor_tensor(out=weighted[:, :].rearrange("p (k c) -> p k c", k=B),
                                         in0=psU[j % 2][:, :].rearrange("p (k c) -> p k c", k=B), scalar=0.0,
                                         in1=a_relu[:, :].rearrange("p (o c) -> p o c", o=1).to_broadcast([P, B, C]),
                                         op0=ALU.max, op1=ALU.mult).then_inc(relu_done, 1)

            def reduce(G, j):
                dve.wait_ge(relu_done, number(G) * J + (j + 1))
                dve.tensor_reduce(logits[:, slot(G) // K, :, j * B:j * B + B].rearrange("p h k -> p k h"),
                                  weighted[:, :].rearrange("p (k h c) -> p k h c", k=B, h=HEADS), AX.X, ALU.add) \
                    .then_inc(reduced, 1)

            def add_linear(G):
                dve.wait_ge(reduced, number(G) * J + J)
                at = logits[:, slot(G) // K, :, :].rearrange("p h k -> p (h k)")
                dve.tensor_tensor(at, at, psL[:, 0:P], ALU.add).then_inc(logits_ready, 1)

            def flat(t, back=False):
                t = t.rearrange("o h s -> o (h s)")
                return t[:, ::-1] if back else t

            def scan_tiles(Q):
                q = number(Q)
                dve.wait_ge(flags_in[parity(Q)], (half(Q) + 1) * (16 * (2 * HEADS + 2)))
                dve.wait_ge(logitsT, q + 1)
                dve.tensor_tensor_scan(scan_a[:, :], starts[:, parity(Q), 0:P], psA[:, 0:P], -BIG, ALU.add, ALU.max).then_inc(scan1, 1)
                dve.wait_ge(scan1, q + 1)
                dve.tensor_tensor_scan(scan_b[:, ::-1], starts[:, parity(Q), 1:P + 1][:, ::-1], scan_a[:, ::-1], -BIG,
                                       ALU.add, ALU.max).then_inc(scan2, 1)

            def scan_group(Q):
                q = number(Q)
                dve.wait_ge(rows_ps, q + 1)
                dve.tensor_copy(last_max[:, :, 0:1], up[:, :, K:SLOTS]).then_inc(rows_sb, 1)
                dve.tensor_copy(last_max[:, :, 1:SLOTS], psB[0:1, 0:P].rearrange("o (h k) -> o h k", k=K)).then_inc(rows_sb, 1)
                dve.tensor_copy(first_max[:, :, 0:K], psB[0:1, P:2 * P].rearrange("o (h k) -> o h k", k=K)).then_inc(rows_sb, 1)
                dve.wait_ge(rows_sb, q * 3 + 3)
                dve.tensor_tensor_scan(flat(up[:, :, :]), flat(through[0:1, parity(Q), 0]), flat(last_max[:, :, :]), -BIG,
                                       ALU.add, ALU.max).then_inc(scan_up, 1)
                dve.tensor_tensor_scan(flat(down[:, :, :], True), flat(through[0:1, parity(Q), 1], True), flat(first_max[:, :, :], True),
                                       -BIG, ALU.add, ALU.max).then_inc(scan_up, 1)
                dve.wait_ge(scan_up, q * 2 + 2)
                dve.tensor_copy(updown[:, 0, :].rearrange("o (h k) -> o h k", k=K), up[:, :, 0:K]).then_inc(updown_sb, 1)
                dve.tensor_copy(updown[:, 1, :].rearrange("o (h k) -> o h k", k=K), down[:, :, 1:SLOTS]).then_inc(updown_sb, 1)

            def scan_again(Q):
                q = number(Q)
                dve.wait_ge(updown_ps, q + 1)
                dve.tensor_tensor_scan(scan_a[:, :], starts[:, parity(Q), 0:P], psA[:, 0:P], psB[:, 256:257], ALU.add, ALU.max).then_inc(scan3, 1)
                dve.wait_ge(scan3, q + 1)
                dve.tensor_tensor_scan(scan_b[:, ::-1], starts[:, parity(Q), 1:P + 1][:, ::-1], scan_a[:, ::-1], psB[:, 257:258],
                                       ALU.add, ALU.max).then_inc(scan4, 1)

            def subtract_max(Q):
                q = number(Q)
                dve.wait_ge(maxT, q + 1)
                dve.tensor_tensor(shift[:, 0, :], last_max[:, :, 0], psA[0:1, P:2 * P].rearrange("o (h k) -> o h k", k=K)[:, :, 0],
                                  ALU.subtract).then_inc(shift1, 1)
                if not early(Q, 1):
                    dve.wait_ge(weights_ready, q)
                dve.tensor_tensor(below[:, :], logits[:, slot(Q) // K, :, :].rearrange("p h k -> p (h k)"), psA[:, P:2 * P],
                                  ALU.subtract).then_inc(below_ready, 1)
                dve.wait_ge(shift1, q + 1)
                dve.tensor_scalar(shift[:, 1, :], shift[:, 0, :], 0.0, None, ALU.min).then_inc(shift2, 1)

            tile_of = [0] * K

            def node_tiles(G):
                _, values = nc.values_load_multi_w_load_instructions(
                    node_tile_row[0:1, ds(number(G) * K, K)], [mybir.EngineType.DVE], min_val=0, max_val=NA - 1,
                    skip_runtime_bounds_check_because="a step's node tile is at most NT")
                tile_of[:] = values

            def scale_first(Q):
                q = number(Q)
                dve.wait_ge(rescale_sb, q + 1)
                if not early(Q, 1):
                    dve.wait_ge(added, q * K)
                tile = ds(tile_of[0], 1)
                num = acc[:, tile, :, 0:C].rearrange("p o e (h c) -> p (o e) h c", h=HEADS)
                den = acc[:, tile, :, C:WX].rearrange("p o e h -> p (o e) h")
                dve.tensor_tensor(num, num, rescale[:, parity(Q), :].rearrange("p (e h o) -> p e h o", e=1, o=1).to_broadcast([P, 2, HEADS, CH]),
                                  ALU.mult).then_inc(rescaled, 1)
                dve.tensor_tensor(den, den, rescale[:, parity(Q), :].rearrange("p (e h) -> p e h", e=1).to_broadcast([P, 2, HEADS]),
                                  ALU.mult).then_inc(rescaled, 1)

            def messages(Q, j):
                if j == 0:
                    dve.wait_ge(weights_ready, number(Q) + 1)
                s0 = slot(Q) + j * B
                hi = rows[:, s0:s0 + B, 0:C].rearrange("p k (h c) -> p k h c", h=HEADS)
                dve.tensor_tensor(hi, hi, rows[:, s0:s0 + B, C:WX].rearrange("p k (h o) -> p k h o", o=1).to_broadcast([P, B, HEADS, CH]),
                                  ALU.mult).then_inc(msg_ready, 1)

            def add(Q, k, width, summed, done):
                q = number(Q)
                if k % 2 == 0:
                    dve.wait_ge(summed, q * (K // 2) + (k // 2 + 1))
                if not (early(Q, 1) and k < 2):
                    dve.wait_ge(done, q * K + (k - 1))
                at = acc[:, ds(tile_of[k], 1), k % 2, 0:width].rearrange("p o w -> p (o w)")
                dve.tensor_tensor(at, at, psP[k // 2 % 2][:, k % 2 * 256:k % 2 * 256 + width], ALU.add).then_inc(done, 1)

            def weave(G, spreads=True, chain=True, middle=True, summing=True):
                Q, O, L = (near(G, n) for n in (-1, -2, -3))
                if spreads:
                    next_idx(near(G, 3), idx_ready)
                    next_local(near(G, 1))
                for j in range(J):
                    if summing:
                        if j == 0:
                            node_tiles(L)
                            scale_first(L)
                            dve.wait_ge(rescaled, number(L) * 2 + 2)
                        for k in range(j * B, j * B + B):
                            add(L, k, WX, sums_ps, added)
                        if j == 0:
                            messages(L, 3)
                    if j == 1 and middle:
                        subtract_max(O)
                    if j == 1 and chain:
                        scan_tiles(Q)
                    if j == 2 and chain:
                        scan_group(Q)
                    if j == 3 and chain:
                        scan_again(Q)
                    if j == 3 and middle:
                        dve.wait_ge(rescale_ps, number(O) + 1)
                        dve.tensor_copy(rescale[:, parity(O), :], psB[:, 264:264 + HEADS]).then_inc(rescale_log, 1)
                    if j == 2 and middle:
                        messages(O, 0)
                        messages(O, 1)
                    if j == 3 and middle:
                        messages(O, 2)
                    if spreads:
                        relu(G, j)
                        reduce(G, j)
                if spreads:
                    add_linear(G)

            dve.wait_ge(fills2, 1)
            groups(dve, lambda G: weave(G, chain=not early(G, 1), middle=not early(G, 2), summing=not early(G, 3)))
            weave(last_group(1), spreads=False)
            weave(last_group(2), spreads=False, chain=False)
            weave(last_group(3), spreads=False, chain=False, middle=False)

            def final(rnd):
                v = fin_v[rnd]
                ops = 4 if rnd == 0 else 7
                for c in range(CHUNKS + 1):
                    if c < CHUNKS:
                        n = c * ops
                        f, w = fin[:, c % 2], work[:, c % 2]
                        tiles = slice(c * CT, (c + 1) * CT)
                        dve.wait_ge(fin_merged[rnd], c + 1)
                        if rnd == 0:
                            dve.tensor_scalar(f[:, 0], acc[:, tiles, 0, C:WX], 1e-30, None, ALU.max).then_inc(v, 1)
                            dve.wait_ge(v, n + 1)
                            dve.reciprocal(f[:, 1], f[:, 0]).then_inc(v, 1)
                            dve.wait_ge(v, n + 2)
                            dve.tensor_tensor(w.rearrange("p t (h c) -> p t h c", h=HEADS),
                                              acc[:, tiles, 0, 0:C].rearrange("p t (h c) -> p t h c", h=HEADS),
                                              f[:, 1].rearrange("p t (h o) -> p t h o", o=1).to_broadcast([P, CT, HEADS, CH]),
                                              ALU.mult).then_inc(v, 1)
                            dve.wait_ge(v, n + 3)
                            dve.tensor_tensor(x_sb[:, tiles, :], x_sb[:, tiles, :], w, ALU.add).then_inc(v, 1)
                        else:
                            count, top, part, inverse, keep, share = acc[:, tiles, 0, C], *(f[:, i, :, 0] for i in range(5))
                            dve.tensor_scalar(top, count, EPS_COUNT, None, ALU.max).then_inc(v, 1)
                            dve.tensor_scalar(part, count, EPS_COUNT, MIX, ALU.is_gt, ALU.mult).then_inc(v, 1)
                            dve.wait_ge(v, n + 2)
                            dve.reciprocal(inverse, top).then_inc(v, 1)
                            dve.tensor_scalar(keep, part, -1.0, 2.0, ALU.mult, ALU.add).then_inc(v, 1)
                            dve.wait_ge(v, n + 4)
                            dve.tensor_tensor(share, inverse, part, ALU.mult).then_inc(v, 1)
                            dve.wait_ge(v, n + 5)
                            dve.tensor_tensor(w, acc[:, tiles, 0, 0:C], f[:, 4, :, 0:1].to_broadcast([P, CT, C]), ALU.mult).then_inc(v, 1)
                            dve.wait_ge(v, n + 6)
                            for i in range(CT):
                                xt = x_sb[:, c * CT + i, :]
                                op = dve.scalar_tensor_tensor(out=xt, in0=xt, scalar=f[:, 3, i, 0:1], in1=w[:, i, :],
                                                              op0=ALU.mult, op1=ALU.add)
                            op.then_inc(v, 1)
                        dve.wait_ge(v, n + ops)
                        for i in range(CT):
                            op = dve.bn_stats(stats[:, i, :], x_sb[:, c * CT + i, :])
                        op.then_inc(fin_stats[rnd], 1)
                        dve.wait_ge(fin_stats[rnd], c + 1)
                        if c >= 2:
                            dve.wait_ge(fin_act[rnd], (c - 1) * ACT_TILES)
                            dve.wait_ge(fin_dve[rnd], (c - 1) * (CT - ACT_TILES))
                        for i in range(CT):
                            op = dve.bn_aggr(mv[:, c % 2, i, :], stats[:, i, :])
                        op.then_inc(fin_var[rnd], 1)
                    if c >= 1:
                        m, s = mv[:, (c - 1) % 2], rstd[:, (c - 1) % 2]
                        dve.wait_ge(fin_std[rnd], c)
                        dve.reciprocal(s[:, 1, :], s[:, 0, :]).then_inc(fin_inv[rnd], 1)
                        dve.wait_ge(fin_inv[rnd], c)
                        dve.scalar_tensor_tensor(out=s[:, 2, :], in0=m[:, :, 0], scalar=-1.0, in1=s[:, 1, :],
                                                 op0=ALU.mult, op1=ALU.mult).then_inc(fin_rs[rnd], 1)
                        for i in range(ACT_TILES, CT):
                            xt = x_sb[:, (c - 1) * CT + i, :]
                            dve.tensor_scalar(xt, xt, m[:, i, 0:1], s[:, 1, i:i + 1], ALU.subtract, ALU.mult).then_inc(fin_dve[rnd], 1)

            fin_inv = sems("fin_inv0 fin_inv1")
            dve.wait_ge(added, NS)
            final(0)

            dve.memset(acc[:, :, 0, :], 0.0).then_inc(acc1_zero, 1)
            dve.memset(rows[:, :, C:C + 1], 1.0).then_inc(acc1_zero, 1)
            dve.wait_ge(acc1_zero, 2)
            dve.wait_ge(S_ready, NS // B + J)

            def onehot1(G, j):
                if not early(G, RING):
                    dve.wait_ge(sums1_ps, number(G) * (2 * J) + (2 * (j + 1) - 2 * RING * J))
                for k in range(j * B, j * B + B):
                    op = dve.tensor_scalar(S[:, slot(G) + k, :], neg_iota[:, :], neg_local_g[:, parity(G), k:k + 1],
                                           weight_g[:, parity(G), k:k + 1], ALU.is_equal, ALU.mult)
                op.then_inc(S1_ready, 1)

            def weave1(G):
                g = number(G)
                next_idx(near(G, 3), idx1_ready)
                dve.tensor_copy(neg_local_g[:, parity(G), :], neg_local[:, ds(g * K, K)]).then_inc(local1_ready, 1)
                dve.tensor_copy(weight_g[:, parity(G), :], weight[:, ds(g * K, K)]).then_inc(local1_ready, 1)
                node_tiles(G)
                dve.wait_ge(local1_ready, g * 2 + 2)
                for j in range(J):
                    onehot1(G, j)
                if early(G, 1):
                    dve.wait_ge(acc1_odd_zero, 1)
                for k in range(K):
                    add(G, k, W1, sums1_ps, added1)

            for g in range(3):
                next_idx((0, g), idx1_ready)
            groups(dve, weave1)
            dve.wait_ge(added1, NS)
            final(1)


_INS = ["x", "src", "dst", "edge_weight", "L0_gnn_w1", "L0_gnn_w2", "L0_gnn_a"]


def kernel(**inputs):
    import numpy as _np
    import concourse.bacc as _bacc
    from concourse import mybir as _mybir
    from concourse.bass_utils import run_bass_kernel_spmd as _run

    nc = _bacc.Bacc("TRN2", target_bir_lowering=False, num_devices=1)
    arrays, args = {}, []
    for name in _INS:
        v = _np.ascontiguousarray(inputs[name])
        arrays[f"in_{name}"] = v
        args.append(nc.dram_tensor(f"in_{name}", v.shape, _mybir.dt.from_np(v.dtype), kind="ExternalInput").ap())
    args.append(nc.dram_tensor("out_0", inputs["x"].shape, _mybir.dt.float32, kind="ExternalOutput").ap())
    graph_kernel(nc, *args)
    r = _run(nc, [arrays], core_ids=[0])
    return r.results[0]["out_0"]
```

```python
import concourse.bass as bass
from concourse import mybir
from contextlib import ExitStack


def graph_kernel(nc, x, src, dst, edge_weight, w1, w2, a, out):
    fp32, bf16, i32, i16 = mybir.dt.float32, mybir.dt.bfloat16, mybir.dt.int32, mybir.dt.int16
    ALU, ACT, AX = mybir.AluOpType, mybir.ActivationFunctionType, mybir.AxisListType
    ds = bass.ds

    P = 128
    N, C = x.shape
    E = src.shape[0]
    HEADS, CH = 8, 16
    SLOPE, MIX = 0.3, 0.3
    EPS_COUNT, EPS_NORM = 1e-8, 1e-5
    ET, NT = -(-E // P), -(-N // P)
    K = 16
    NG = -(-(ET + NT - 1) // K)
    NS = NG * K
    SM = NS // P
    NA = NT + 1
    B, J = 4, K // 4
    RING = 4
    QW = NS // 4
    FULL_E, TAIL_E = E // P, E % P
    FULL_N, TAIL_N = N // P, N % P
    WX = C + HEADS
    W1 = C + 1
    SLOTS = K + 1
    BIG = 1e30
    NO_NODE = 1000000
    CT = 7
    CHUNKS = NT // CT
    XB = 4
    BLOCKS = -(-NT // XB)
    PAIRS = -(-NT // 2)
    X_CUTS = [XB, 3 * XB, 6 * XB, FULL_N, NT]
    assert NS % P == 0 and NT % CT == 0 and K * HEADS == P and TAIL_E and TAIL_N
    assert NG % RING == 0 and BLOCKS * XB <= RING * K

    def dram(name, shape, dt):
        return nc.dram_tensor(name, shape, dt, kind="Internal").ap()

    edge_rows = dram("edge_rows", [ET, 3 * P], i32)
    hi_rows = dram("hi_rows", [NT * P, WX], fp32)
    x1_rows = dram("x1_rows", [NT * P, C], fp32)
    locals_flat = dram("locals_flat", [1 + NS * P], fp32)
    starts_flat = dram("starts_flat", [NS * P + P], fp32)
    through_flat = dram("through_flat", [2, NS], fp32)

    ctx = ExitStack()
    with ctx:
        def sb(name, shape, dt=fp32):
            return ctx.enter_context(nc.sbuf_tensor(name, shape, dt))

        def ps(name, shape=(P, 512), dt=fp32):
            return ctx.enter_context(nc.psum_tensor(name, list(shape), dt))

        def sem(name):
            return ctx.enter_context(nc.semaphore(name))

        def sems(names):
            return [sem(n) for n in names.split()]

        neg_iota = sb("neg_iota", [P, P])
        tile_no = sb("tile_no", [P, SM])
        step_no = sb("step_no", [P, SM])
        ident = sb("ident", [P, P])
        ones_bf = sb("ones_bf", [P, P], bf16)
        a_relu = sb("a_relu", [P, C])
        pads = sb("pads", [1, 3, P], i32)
        eps_col = sb("eps_col", [P, 1])
        one_col = sb("one_col", [P, 1])
        last_dst = sb("last_dst", [P, SM], i32)
        last_tile = sb("last_tile", [P, SM], i32)
        ends_at = sb("ends_at", [P, SM])
        node_tile_row = sb("node_tile_row", [1, NS + K], i16)
        edge_tile_col = sb("edge_tile_col", [P, SM], i32)
        first_node = sb("first_node", [P, SM])
        src_idx = sb("src_idx", [P, NS + 3 * K], i16)
        neg_local = sb("neg_local", [P, NS + K], bf16)
        weight = sb("weight", [P, NS])
        x_sb = sb("x_sb", [P, NT, C])
        hj = sb("hj", [P, NA, WX])
        acc = sb("acc", [P, NA, 2, WX])
        idx_g = sb("idx_g", [P, RING, K], i32)
        rows = sb("rows", [P, RING * K, WX])
        S = sb("S", [P, RING * K, P])
        logits = sb("logits", [P, RING, HEADS, K])
        neg_local_g = sb("neg_local_g", [P, 2, K])
        weight_g = sb("weight_g", [P, 2, K])
        starts = sb("starts", [P, 2, P + 1])
        through = sb("through", [1, 2, 2, HEADS, SLOTS])
        rescale = sb("rescale", [P, 2, HEADS])
        ST = sb("ST", [P, 2, B * P])
        weighted = sb("weighted", [P, B * P])
        scan_a = sb("scan_a", [P, P])
        scan_b = sb("scan_b", [P, P])
        last_max = sb("last_max", [1, HEADS, SLOTS])
        first_max = sb("first_max", [1, HEADS, SLOTS])
        up = sb("up", [1, HEADS, SLOTS])
        down = sb("down", [1, HEADS, SLOTS])
        updown = sb("updown", [1, 2, P])
        shift = sb("shift", [1, 2, HEADS])
        below = sb("below", [P, P])
        stats = sb("stats", [P, CT, 6])
        mv = sb("mv", [P, 2, CT, 2])
        rstd = sb("rstd", [P, 2, 3, CT])
        small = sb("small", [P, 4, SM])
        w12 = logits[:, :, :, :].rearrange("p r h k -> p (r h k)")[:, 0:2 * WX].rearrange("p (a w) -> p a w", a=2)
        a_rep = scan_a
        tab_f = weighted[:, :].rearrange("p (a q e) -> p a q e", a=2, q=2)

        flat_S = S[:, :, :].rearrange("p k n -> p (k n)")
        passed = flat_S[:, 0:NS].bitcast(bf16).rearrange("p (a s) -> p a s", a=2)
        iota = flat_S[:, NS:2 * NS]
        local_s = flat_S[:, 0:SM * P].rearrange("p (m e) -> p m e", m=SM)
        prev_s = flat_S[:, SM * P:2 * SM * P].rearrange("p (m e) -> p m e", m=SM)
        TR = 12
        tables = flat_S[:, 2 * NS:2 * NS + TR * 3 * P].bitcast(i32).rearrange("p (m q e) -> p m q e", m=TR, q=3)
        edge_tile_row = weight[0:1, :]
        work = rows[:, :, :].rearrange("p k w -> p (k w)")[:, 0:2 * CT * C].rearrange("p (b t c) -> p b t c", b=2, t=CT)
        fin = rows[:, :, :].rearrange("p k w -> p (k w)")[:, 2 * CT * C:2 * CT * C + 6 * NT].rearrange("p (i t) -> p i t", i=6)

        psU = [ps("psU0", (P, B, 256)), ps("psU1", (P, B, 256))]
        psT = ps("psT")
        psP = [ps("psP0"), ps("psP1")]
        psC = ps("psC")
        C_LOGITS, C_MAX, C_ENDS, C_UPDOWN, C_SHIFT = 0, P, P, 3 * P, 3 * P + 8

        *quarters, xT_bank = (u[:, i:i + 2, :].rearrange("p k w -> p (k w)") for u in psU for i in (0, 2))
        quarters[3:] = [psT]

        consts, memsets, fills, fills2 = sems("consts memsets fills fills2")
        w_in, last_in, rows_made = sems("w_in last_in rows_made")
        x_in = [sem(f"x_in{i}") for i in range(len(X_CUTS))]
        pre, w_ready = sems("pre w_ready")
        passed_ready, passed_used, tiles_row, col_ps, col_ready = sems(
            "passed_ready passed_used tiles_row col_ps col_ready")
        xT_ps, xT_sb, hi_ps, hi_sb, hj_ps, hj_sb = sems("xT_ps xT_sb hi_ps hi_sb hj_ps hj_sb")
        hi_out = sem("hi_out")
        table_in = [sem(f"table_in{m}") for m in range(TR)]
        tab_ready, tab_ps, tab_out, local_out = sems("tab_ready tab_ps tab_out local_out")
        locals_out, prev_in, starts_out, next_in, through_out = sems(
            "locals_out prev_in starts_out next_in through_out")
        starts_made, through_made, node_tiles_ready = sems("starts_made through_made node_tiles_ready")
        idx_ready, neg_ready = sems("idx_ready neg_ready")
        rows_in = [[sem(f"rows_in{p}{j}") for j in range(J)] for p in range(RING)]
        flags_in = [sem("flags_in0"), sem("flags_in1")]
        square_done, S_ready, ST_ps, ST_sb, U_ready, relu_done, reduced, logits_ready = sems(
            "square_done S_ready ST_ps ST_sb U_ready relu_done reduced logits_ready")
        logitsT, scan1, scan2, ends_ps, ends_sb, carry_sb, scan_up, updown_sb, updown_ps, scan3, scan4, maxT = sems(
            "logitsT scan1 scan2 ends_ps ends_sb carry_sb scan_up updown_sb updown_ps scan3 scan4 maxT")
        shift1, shift2, below_ready, weights_ready, rescale_ps, rescale_log, rescale_sb, rescaled = sems(
            "shift1 shift2 below_ready weights_ready rescale_ps rescale_log rescale_sb rescaled")
        msg_ready, sums_ps, added = sems("msg_ready sums_ps added")
        idx1_ready, local1_ready, S1_ready, sums1_ps, added1 = sems(
            "idx1_ready local1_ready S1_ready sums1_ps added1")
        rows1_in = [[sem(f"rows1_in{p}{j}") for j in range(J)] for p in range(RING)]
        fin_merged, fin_small, fin_w, fin_x, fin_stats, fin_var, fin_std, fin_inv, fin_rs, fin_done = (
            [sem(f"{n}{rnd}") for rnd in range(2)] for n in
            "fin_merged fin_small fin_w fin_x fin_stats fin_var fin_std fin_inv fin_rs fin_done".split())
        x1_out, out_done, acc1_zero, acc1_odd_zero = sems("x1_out out_done acc1_zero acc1_odd_zero")
        passed_by = {e: sem(f"passed_by_{e}") for e in ("pe", "pool")}

        block = ctx.enter_context(nc.Block())

        def number(G):
            return G[0] * RING + G[1]

        def half(G):
            return G[0] * (RING // 2) + G[1] // 2

        def lap(G):
            return G[0] + G[1] // RING

        def slot(G):
            return G[1] % RING * K

        def parity(G):
            return G[1] % 2

        def near(G, n):
            return G[0], G[1] + n

        def early(G, n):
            return isinstance(G[0], int) and number(G) < n

        def groups(engine, one):
            for g in range(RING):
                one((0, g))
            with engine.Fori(0, NG // RING - 1) as it:
                base = engine.snap(it + 1)
                for step in range(RING):
                    one((base, step))

        def last_group(n=0):
            return 0, NG - 1 + n

        def block_tiles(m):
            return range(m * XB, min(m * XB + XB, NT))

        def pair_tiles(n):
            return range(2 * n, min(2 * n + 2, NT))

        def chunk(c):
            return slice(c * CT, (c + 1) * CT)

        @block.sync
        def _(sp):
            sp.wait_ge(memsets, 3)
            tiles = dst[0:FULL_E * P].rearrange("(i e) -> i e", e=P)[:, P - 1:P]
            whole = FULL_E // SM
            with nc.allow_non_contiguous_dma(reason="one element of each edge tile"):
                sp.dma_start(last_dst[0:whole, :],
                             tiles[0:whole * SM, :].rearrange("(p c) o -> p (c o)", c=SM)).then_inc(last_in, 16)
                sp.dma_start(last_dst[whole:whole + 1, 0:FULL_E - whole * SM],
                             tiles[whole * SM:FULL_E, :].rearrange("(p c) o -> p (c o)", p=1)).then_inc(last_in, 16)
            sp.wait_ge(fills, 1)
            for i, (t0, t1) in enumerate(zip([0] + X_CUTS, X_CUTS)):
                if t1 <= FULL_N:
                    sp.dma_start(x_sb[:, t0:t1, :], x[t0 * P:t1 * P, :].rearrange("(t p) c -> p t c", p=P)).then_inc(x_in[i], 16)
                else:
                    sp.dma_start(x_sb[0:TAIL_N, t0, :], x[t0 * P:N, :]).then_inc(x_in[i], 16)
                if i == 0:
                    sp.dma_start(w12[:, 0, 0:C], w1).then_inc(w_in, 16)
                    sp.dma_start(w12[:, 1, 0:C], w2).then_inc(w_in, 16)
                    sp.dma_start(a_rep[:, :], a[0, :].partition_broadcast(P)).then_inc(w_in, 16)
            even = FULL_E // 16 * 16
            for q, v in enumerate((src, dst, edge_weight.bitcast(i32))):
                full = v[0:FULL_E * P].rearrange("(i e) -> i e", e=P)
                sp.dma_start(edge_rows[0:even, q * P:q * P + P], full[0:even, :]).then_inc(rows_made, 16)
                sp.dma_start(edge_rows[even:FULL_E, q * P:q * P + P], full[even:FULL_E, :]).then_inc(rows_made, 16)
                sp.dma_start(edge_rows[FULL_E:ET, q * P:q * P + TAIL_E],
                             v[FULL_E * P:E].rearrange("(o e) -> o e", o=1)).then_inc(rows_made, 16)
                sp.dma_start(edge_rows[FULL_E:ET, q * P + TAIL_E:q * P + P], pads[:, q, TAIL_E:P]).then_inc(rows_made, 16)
            for m in range(BLOCKS):
                ts = block_tiles(m)
                sp.wait_ge(hi_sb, ts[-1] // 2 + 1)
                s0 = m * XB
                sp.dma_start(hi_rows[ts[0] * P:(ts[-1] + 1) * P, :].rearrange("(t p) c -> p t c", p=P),
                             rows[:, s0:s0 + len(ts), :]).then_inc(hi_out, 16)
            flat = locals_flat[1:1 + NS * P].rearrange("(m p e) -> p m e", p=P, e=P)
            sp.dma_start(locals_flat[0:1].rearrange("(o e) -> o e", o=1), eps_col[0:1, 0:1]).then_inc(locals_out, 16)
            sp.wait_ge(tab_ready, 2 * SM)
            sp.dma_start(flat, local_s).then_inc(locals_out, 16)
            sp.wait_ge(locals_out, 32)
            sp.dma_start(prev_s, locals_flat[0:NS * P].rearrange("(m p e) -> p m e", p=P, e=P)).then_inc(prev_in, 16)
            sp.wait_ge(starts_made, 1)
            sp.dma_start(starts_flat[0:NS * P].rearrange("(m p e) -> p m e", p=P, e=P), prev_s).then_inc(starts_out, 16)
            sp.dma_start(starts_flat[NS * P:NS * P + 1].rearrange("(o e) -> o e", o=1), small[0:1, 3, 0:1]).then_inc(starts_out, 16)
            sp.wait_ge(starts_out, 32)
            with nc.allow_non_contiguous_dma(reason="one element of each step"):
                sp.dma_start(small[:, 0, :].rearrange("p (m o) -> p m o", o=1),
                             starts_flat[P:P + NS * P].rearrange("(m p e) -> p m e", p=P, e=P)[:, :, 0:1]).then_inc(next_in, 16)
                sp.wait_ge(through_made, 2)
                sp.dma_start(through_flat[0, :].rearrange("(m p) -> p m", p=P), small[:, 1, :]).then_inc(through_out, 16)
                sp.dma_start(through_flat[1, :].rearrange("(m p) -> p m", p=P), small[:, 2, :]).then_inc(through_out, 16)
            sp.wait_ge(through_out, 32)

            def flags(G):
                if not early(G, 2):
                    sp.wait_ge(scan4, number(G) - 1)
                part = starts_flat[ds(number(G) * (K * P), K * P + P)]
                for h in range(HEADS):
                    sp.dma_start(starts[h * K:h * K + K, parity(G), 0:P], part[0:K * P].rearrange("(k e) -> k e", e=P)) \
                        .then_inc(flags_in[parity(G)], 16)
                    sp.dma_start(starts[h * K:h * K + K, parity(G), P:P + 1],
                                 part[P:K * P + P].rearrange("(k e) -> k e", e=P)[:, 0:1]).then_inc(flags_in[parity(G)], 16)
                for d in range(2):
                    sp.dma_start(through[0:1, parity(G), d, :, 1 - d:1 - d + K],
                                 through_flat[d:d + 1, ds(number(G) * K, K)].rearrange("o (b k) -> o b k", b=1)
                                 .to_broadcast([1, HEADS, K])).then_inc(flags_in[parity(G)], 16)

            with nc.allow_non_contiguous_dma(reason="the next tile's first element"):
                groups(sp, flags)

            for rnd, (table, done) in enumerate(((x1_rows, x1_out), (out, out_done))):
                for c in range(CHUNKS):
                    sp.wait_ge(fin_done[rnd], (c + 1) * CT)
                    t0, t1 = c * CT, (c + 1) * CT
                    if rnd == 1 and c == CHUNKS - 1:
                        t1 = FULL_N
                    sp.dma_start(table[t0 * P:t1 * P, :].rearrange("(t p) c -> p t c", p=P), x_sb[:, t0:t1, :]).then_inc(done, 16)
            sp.dma_start(out[FULL_N * P:N, :], x_sb[0:TAIL_N, FULL_N, :]).then_inc(out_done, 16)
            sp.wait_ge(out_done, 16 * (CHUNKS + 1))

        @block.gpsimd
        def _(pool):
            pool.memset(last_dst[:, :], NO_NODE).then_inc(memsets, 1)
            pool.memset(pads[:, :, :], 0).then_inc(memsets, 1)
            pool.wait_ge(memsets, 2)
            pool.memset(pads[:, 1, :], NO_NODE).then_inc(memsets, 1)
            pool.iota(tile_no[:, :], [[1, SM]], base=0, channel_multiplier=SM,
                      allow_small_or_imprecise_dtypes=True).then_inc(consts, 1)
            pool.memset(ones_bf[:, :], 1.0).then_inc(consts, 1)
            pool.memset(ident[:, :], 0.0).then_inc(consts, 1)
            pool.wait_ge(consts, 3)
            pool.affine_select(out=ident[:, :], in_=ident[:, :], compare_op=ALU.not_equal, fill=1.0,
                               base=0, pattern=[[-1, P]], channel_multiplier=1).then_inc(consts, 1)
            pool.iota(iota, [[1, NS]], base=0, channel_multiplier=0,
                      allow_small_or_imprecise_dtypes=True).then_inc(consts, 1)
            pool.iota(step_no[:, :], [[P, SM]], base=0, channel_multiplier=1,
                      allow_small_or_imprecise_dtypes=True).then_inc(consts, 1)
            pool.iota(neg_iota[:, :], [[-1, P]], base=0, channel_multiplier=0,
                      allow_small_or_imprecise_dtypes=True).then_inc(consts, 1)
            pool.memset(acc[:, :, :, :], 0.0).then_inc(fills2, 1)
            pool.wait_ge(rows_made, 16 * 12)
            pool.wait_ge(col_ready, 1)
            for m in range(SM):
                if m >= TR:
                    pool.wait_ge(tab_ready, 2 * (m - TR + 1))
                    pool.wait_ge(tab_ps, m - TR + 1)
                pool.indirect_dma_start(tables[:, m % TR, :, :].rearrange("p q e -> p (q e)"), None, edge_rows,
                                        bass.IndirectOffsetOnAxis(ap=edge_tile_col[:, m:m + 1], axis=0)) \
                    .then_inc(table_in[m % TR], 16)

            def final(rnd):
                for c in range(CHUNKS + 1):
                    if c < CHUNKS:
                        pool.tensor_tensor(acc[:, chunk(c), 0, 0:C], acc[:, chunk(c), 0, 0:C], acc[:, chunk(c), 1, 0:C], ALU.add) \
                            .then_inc(fin_merged[rnd], 1)
                    if c >= 1 and rnd == 0:
                        pool.wait_ge(fin_w[rnd], c)
                        pool.tensor_tensor(x_sb[:, chunk(c - 1), :], x_sb[:, chunk(c - 1), :], work[:, (c - 1) % 2], ALU.add) \
                            .then_inc(fin_x[rnd], 1)

            pool.wait_ge(hi_out, 16 * BLOCKS)
            for rnd, (table, width, arrived, ready, used) in enumerate((
                    (hi_rows, WX, rows_in, idx_ready, sums_ps), (x1_rows, C, rows1_in, idx1_ready, sums1_ps))):
                if rnd == 1:
                    pool.wait_ge(added, NS)
                    final(0)
                    pool.wait_ge(fin_merged[0], CHUNKS)
                    pool.wait_ge(fin_small[0], 1)
                    pool.memset(acc[:, :, 1, :], 0.0).then_inc(acc1_odd_zero, 1)
                    pool.wait_ge(x1_out, 16 * CHUNKS)

                def gather(G):
                    pool.wait_ge(ready, number(G) + 1)
                    for j in range(J):
                        if not early(G, RING):
                            pool.wait_ge(used, number(G) * (2 * J) + 2 * (j + 1 - RING * J))
                            pool.sem_inc(passed_by["pool"], 1)
                        for k in range(j * B, j * B + B):
                            pool.indirect_dma_start(rows[:, slot(G) + k, 0:width], None, table,
                                                    bass.IndirectOffsetOnAxis(ap=idx_g[:, slot(G) // K, k:k + 1], axis=0)) \
                                .then_inc(arrived[slot(G) // K][j], 16)

                groups(pool, gather)
            pool.wait_ge(added1, NS)
            final(1)

        @block.tensor
        def _(pe):
            pe.wait_ge(consts, 7)

            def turn(m):
                for i, t1 in enumerate(X_CUTS):
                    if t1 > m * XB and (i == 0 or X_CUTS[i - 1] < (m + 1) * XB):
                        pe.wait_ge(x_in[i], 16)
                if m >= 2:
                    pe.wait_ge(xT_sb, m - 1)
                for i, t in enumerate(block_tiles(m)):
                    tr = pe.transpose((psC, xT_bank)[m % 2][:, i * P:i * P + P], x_sb[:, t, :], ident[:, :])
                tr.then_inc(xT_ps, 1)

            def project(n, which, done):
                for i, t in enumerate(pair_tiles(n)):
                    mm = pe.matmul(psP[n % 2][:, i * 256:i * 256 + WX], hj[:, t, 0:C], w12[:, which, :], start=True, stop=True)
                mm.then_inc(done, 1)

            turn(0)
            for m in range(BLOCKS):
                if m + 1 < BLOCKS:
                    turn(m + 1)
                for c in range(2 * m, min(2 * m + 2, SM)):
                    pe.wait_ge(passed_ready, c + 1)
                    for q in range(4):
                        mm = pe.matmul(quarters[q][:, 0:QW], ones_bf[:, :], passed[:, c % 2, q * QW:(q + 1) * QW],
                                       start=(c == 0), stop=(c == SM - 1))
                    mm.then_inc(passed_used, 1)
                if 2 * m > SM and 2 * m - 2 <= SM:
                    pe.wait_ge(tiles_row, 4)
                    for c in range(SM):
                        tr = pe.transpose(psT[:, c:c + 1], edge_tile_row[0:1, c * P:c * P + P], ident[0:1, 0:1])
                    tr.then_inc(col_ps, 1)
                pe.wait_ge(xT_sb, m + 1)
                pe.wait_ge(w_ready, 2)
                for n in range(m * XB // 2, block_tiles(m)[-1] // 2 + 1):
                    if n >= 2:
                        pe.wait_ge(hi_sb, n - 1)
                    project(n, 0, hi_ps)
            for m in range(SM):
                bank = (psT, psC)[m % 2]
                pe.wait_ge(tab_ready, 2 * m + 2)
                pe.wait_ge(table_in[m % TR], 16 * (m // TR + 1))
                if m >= 2:
                    pe.wait_ge(tab_out, m - 1)
                    pe.wait_ge(local_out, m - 1)
                pe.transpose(bank[:, 0:P], tab_f[:, m % 2, 0, :], ident[:, :])
                pe.transpose(bank[:, P:2 * P], local_s[:, m, :], ident[:, :])
                pe.transpose(bank[:, 2 * P:3 * P], tables[:, m % TR, 2, :].bitcast(fp32), ident[:, :]).then_inc(tab_ps, 1)

            pe.wait_ge(hi_sb, PAIRS)
            for n in range(PAIRS):
                if n >= 2:
                    pe.wait_ge(hj_sb, n - 1)
                project(n, 1, hj_ps)
            pe.wait_ge(hj_sb, PAIRS)

            def turn_S(G, j):
                b = number(G) * J + j
                pe.wait_ge(S_ready, b + 1)
                if not (early(G, 1) and j == 0):
                    pe.wait_ge(ST_sb, b)
                for k in range(B):
                    tr = pe.transpose(psT[:, k * P:k * P + P], S[:, slot(G) + j * B + k, :], ident[:, :])
                tr.then_inc(ST_ps, 1)

            tile_of = [0] * K

            def node_tiles(G):
                _, values = nc.values_load_multi_w_load_instructions(
                    node_tile_row[0:1, ds(number(G) * K, K)], [mybir.EngineType.PE], min_val=0, max_val=NA - 1,
                    skip_runtime_bounds_check_because="a step's node tile is at most NT")
                tile_of[:] = values

            def spread(G, j):
                b = number(G) * J + j
                s0 = slot(G) + j * B
                pe.wait_ge(rows_in[slot(G) // K][j], (lap(G) + 1) * (16 * B))
                if not (early(G, 1) and j < 2):
                    pe.wait_ge(logits_ready, b - 1)
                U = psU[j % 2]
                for i in range(2):
                    pe.matmul(U[:, 2 * i:2 * i + 2, 0:WX], ident[:, :], rows[:, s0 + 2 * i:s0 + 2 * i + 2, :],
                              start=True, stop=True, skip_group_check=True)
                pe.wait_ge(ST_sb, b + 1)
                for k in range(B):
                    mm = pe.matmul(U[:, k, 0:WX], ST[:, j % 2, k * P:k * P + P],
                                   hj[:, ds(tile_of[j * B + k], 1), :], start=False, stop=True, skip_group_check=True)
                mm.then_inc(U_ready, 1)

            def turn_logits(Q):
                q = number(Q)
                pe.wait_ge(logits_ready, q * J + J)
                if not early(Q, 1):
                    pe.wait_ge(scan4, q)
                if not early(Q, 2):
                    pe.wait_ge(rescale_log, q - 1)
                    pe.sem_inc(passed_by["pe"], 1)
                pe.transpose(psC[:, C_LOGITS:C_LOGITS + P], logits[:, slot(Q) // K, :, :].rearrange("p h k -> p (h k)"), ident[:, :]).then_inc(logitsT, 1)

            def turn_ends(Q):
                q = number(Q)
                pe.wait_ge(scan2, q + 1)
                pe.transpose(psC[0:1, C_ENDS:C_ENDS + P], scan_b[:, P - 1:P], ident[:, :])
                pe.transpose(psC[0:1, C_ENDS + P:C_ENDS + 2 * P], scan_b[:, 0:1], ident[:, :]).then_inc(ends_ps, 1)

            def turn_updown(Q):
                pe.wait_ge(updown_sb, number(Q) * 2 + 2)
                pe.sem_inc(passed_by["pe"], 1)
                pe.transpose(psC[:, C_UPDOWN:C_UPDOWN + 1], updown[0:1, 0, :], ident[0:1, 0:1])
                pe.transpose(psC[:, C_UPDOWN + 1:C_UPDOWN + 2], updown[0:1, 1, :], ident[0:1, 0:1]).then_inc(updown_ps, 1)

            def turn_max(Q):
                pe.wait_ge(scan4, number(Q) + 1)
                pe.transpose(psC[:, C_MAX:C_MAX + P], scan_b[:, :], ident[:, :]).then_inc(maxT, 1)

            def spread_shift(Q, more):
                if more:
                    pe.wait_ge(ends_sb, number(Q) * 2 + 4)
                    pe.sem_inc(passed_by["pe"], 1)
                pe.wait_ge(shift2, number(Q) + 1)
                pe.matmul(psC[:, C_SHIFT:C_SHIFT + HEADS], S[0:1, slot(Q), :], shift[0:1, 1, :], start=True, stop=True) \
                    .then_inc(rescale_ps, 1)

            def sums(Q, j):
                pe.wait_ge(msg_ready, number(Q) * J + (j + 1))
                for i in range(2):
                    n = (number(Q) * J + j) * 2 + i
                    if not (early(Q, 1) and j == 0):
                        pe.wait_ge(added, n * 2 - 2)
                    for e in range(2):
                        k = j * B + i * 2 + e
                        mm = pe.matmul(psP[i][:, e * 256:e * 256 + WX], S[:, slot(Q) + k, :], rows[:, slot(Q) + k, :],
                                       start=True, stop=True)
                    mm.then_inc(sums_ps, 1)

            def weave(G, spreads=True, chain=True, middle=True, summing=True):
                H, Q, O, L = (near(G, n) for n in (1, -1, -2, -3))
                for j in range(J):
                    if spreads:
                        if j == 0:
                            node_tiles(G)
                        turn_S(G if j + 1 < J else H, (j + 1) % J)
                        spread(G, j)
                    if j + 1 < J and summing:
                        sums(L, j + 1)
                    if j + 1 == J and middle:
                        sums(O, 0)
                    if j == 0 and chain:
                        turn_logits(Q)
                    if j == 0 and middle:
                        turn_max(O)
                    if j == 1 and chain:
                        turn_ends(Q)
                    if j == 2 and middle:
                        spread_shift(O, chain)
                    if j == 2 and chain:
                        turn_updown(Q)

            pe.wait_ge(node_tiles_ready, 2)
            turn_S((0, 0), 0)
            groups(pe, lambda G: weave(G, chain=not early(G, 1), middle=not early(G, 2), summing=not early(G, 3)))
            weave(last_group(1), spreads=False)
            weave(last_group(2), spreads=False, chain=False)
            weave(last_group(3), spreads=False, chain=False, middle=False)

            def sums1(G):
                for j in range(J):
                    pe.wait_ge(rows1_in[slot(G) // K][j], (lap(G) + 1) * (16 * B))
                    pe.wait_ge(S1_ready, number(G) * J + (j + 1))
                    for i in range(2):
                        n = (number(G) * J + j) * 2 + i
                        if not (early(G, 1) and j == 0):
                            pe.wait_ge(added1, n * 2 - 2)
                        for e in range(2):
                            k = slot(G) + j * B + i * 2 + e
                            mm = pe.matmul(psP[i][:, e * 256:e * 256 + W1], S[:, k, :], rows[:, k, 0:W1],
                                           start=True, stop=True)
                        mm.then_inc(sums1_ps, 1)

            pe.wait_ge(acc1_zero, 2)
            groups(pe, sums1)

        @block.scalar
        def _(act):
            def take(n, table, ready, done):
                act.wait_ge(ready, n + 1)
                ts = pair_tiles(n)
                act.activation(table[:, ts[0]:ts[-1] + 1, :],
                               psP[n % 2][:, :].rearrange("p (a w) -> p a w", a=2)[:, 0:len(ts), 0:WX], ACT.Copy).then_inc(done, 1)

            for m in range(BLOCKS):
                ts = block_tiles(m)
                act.wait_ge(xT_ps, m + 1)
                act.activation(hj[:, ts[0]:ts[-1] + 1, 0:C], (psC, xT_bank)[m % 2][:, 0:len(ts) * P].rearrange("p (a c) -> p a c", c=C),
                               ACT.Copy).then_inc(xT_sb, 1)
                for n in range(m * XB // 2, ts[-1] // 2 + 1):
                    take(n, rows, hi_ps, hi_sb)
            for n in range(PAIRS):
                take(n, hj, hj_ps, hj_sb)

            def onehot(G, j):
                g = number(G)
                act.wait_ge(neg_ready, g + 1)
                if not early(G, RING):
                    act.wait_ge(sums_ps, g * (2 * J) + (2 * (j + 1) - 2 * RING * J))
                s0 = slot(G) + j * B
                for k in range(B):
                    op = act.activation(S[:, s0 + k, :], neg_iota[:, :], ACT.Square, scale=-1.0,
                                        bias=neg_local_g[:, parity(G), j * B + k:j * B + k + 1])
                op.then_inc(square_done, 1)
                act.wait_ge(square_done, g * J + (j + 1))
                act.activation(S[:, s0:s0 + B, :], S[:, s0:s0 + B, :], ACT.Relu, scale=-1.0, bias=one_col[:, :]).then_inc(S_ready, 1)

            def copy_ST(G, j):
                b = number(G) * J + j
                act.wait_ge(ST_ps, b + 1)
                if not (early(G, 1) and j < 2):
                    act.wait_ge(U_ready, b - 1)
                act.activation(ST[:, j % 2, :], psT[:, :], ACT.Copy).then_inc(ST_sb, 1)

            def exps(Q):
                q = number(Q)
                act.wait_ge(below_ready, q + 1)
                act.activation(rows[:, slot(Q):slot(Q) + K, C:WX].rearrange("p k h -> p h k"),
                               below[:, :].rearrange("p (h k) -> p h k", k=K), ACT.Exp).then_inc(weights_ready, 1)

            def copy_ends(Q):
                q = number(Q)
                act.wait_ge(ends_ps, q + 1)
                if not early(Q, 1):
                    act.wait_ge(below_ready, q)
                act.activation(last_max[:, :, 1:SLOTS], psC[0:1, C_ENDS:C_ENDS + P].rearrange("o (h k) -> o h k", k=K), ACT.Copy).then_inc(ends_sb, 1)
                act.activation(first_max[:, :, 0:K], psC[0:1, C_ENDS + P:C_ENDS + 2 * P].rearrange("o (h k) -> o h k", k=K), ACT.Copy).then_inc(ends_sb, 1)

            def copy_updown(Q):
                act.wait_ge(scan_up, number(Q) * 2 + 2)
                act.activation(updown[:, 0, :].rearrange("o (h k) -> o h k", k=K), up[:, :, 0:K], ACT.Copy).then_inc(updown_sb, 1)
                act.activation(updown[:, 1, :].rearrange("o (h k) -> o h k", k=K), down[:, :, 1:SLOTS], ACT.Copy).then_inc(updown_sb, 1)

            def exp_shift(Q):
                act.wait_ge(rescale_log, number(Q) + 1)
                act.activation(rescale[:, parity(Q), :], rescale[:, parity(Q), :], ACT.Exp).then_inc(rescale_sb, 1)

            def weave(G):
                H, Q, O = near(G, 1), near(G, -1), near(G, -2)
                copy_ST(G, 1)
                onehot(H, 0)
                copy_ST(G, 2)
                if not early(G, 2):
                    exps(O)
                if not early(G, 1):
                    copy_ends(Q)
                onehot(H, 1)
                if not early(G, 1):
                    copy_updown(Q)
                copy_ST(G, 3)
                onehot(H, 2)
                copy_ST(H, 0)
                if not early(G, 2):
                    exp_shift(O)
                onehot(H, 3)

            act.wait_ge(through_made, 2)
            act.wait_ge(starts_out, 32)
            for j in range(J):
                onehot((0, 0), j)
                if j == 0:
                    copy_ST((0, 0), 0)
            groups(act, weave)
            exps(last_group(-1))
            copy_ends(last_group())
            copy_updown(last_group())
            exp_shift(last_group(-1))
            exps(last_group())
            exp_shift(last_group())

            for rnd in range(2):
                for c in range(CHUNKS + 1):
                    if c < CHUNKS:
                        act.wait_ge(fin_var[rnd], c + 1)
                        act.activation(rstd[:, c % 2, 0, :], mv[:, c % 2, :, 1], ACT.Sqrt, bias=eps_col[:, :]).then_inc(fin_std[rnd], 1)
                    if c >= 1:
                        act.wait_ge(fin_rs[rnd], c)
                        for i in range(CT):
                            xt = x_sb[:, (c - 1) * CT + i, :]
                            act.activation(xt, xt, ACT.Identity, bias=rstd[:, (c - 1) % 2, 2, i:i + 1],
                                           scale=rstd[:, (c - 1) % 2, 1, i:i + 1]).then_inc(fin_done[rnd], 1)

        @block.vector
        def _(dve):
            dve.memset(x_sb[:, FULL_N:NT, :], 0.0).then_inc(fills, 1)
            dve.memset(eps_col[:, :], EPS_NORM).then_inc(fills, 1)
            dve.memset(one_col[:, :], 1.0).then_inc(fills, 1)
            dve.memset(small[:, 3, :], -BIG).then_inc(fills, 1)
            dve.memset(up[:, :, :], -BIG).then_inc(fills, 1)
            dve.memset(first_max[:, :, :], -BIG).then_inc(fills, 1)
            dve.wait_ge(last_in, 32)
            dve.wait_ge(consts, 7)
            dve.tensor_scalar(last_tile[:, :], last_dst[:, :], P.bit_length() - 1, None, ALU.logical_shift_right).then_inc(pre, 1)
            dve.wait_ge(pre, 1)
            dve.tensor_tensor(ends_at[:, :], last_tile[:, :], tile_no[:, :], ALU.add).then_inc(pre, 1)
            dve.wait_ge(pre, 2)

            def compare(c):
                if c >= 2:
                    dve.wait_ge(passed_used, c - 1)
                dve.tensor_scalar(passed[:, c % 2, :], iota, ends_at[:, c:c + 1], None, ALU.is_gt).then_inc(passed_ready, 1)

            compare(0)
            compare(1)
            dve.wait_ge(w_in, 48)
            for i in range(2):
                dve.tensor_tensor(weighted[:, i * C:i * C + C], w12[:, i, 0:C], a_rep[:, :], ALU.mult).then_inc(pre, 1)
            dve.tensor_scalar(a_relu[:, :], a_rep[:, :], 1.0 - SLOPE, None, ALU.mult).then_inc(pre, 1)
            dve.wait_ge(pre, 5)
            for i in range(2):
                dve.tensor_reduce(w12[:, i, C:WX], weighted[:, i * C:i * C + C].rearrange("p (h c) -> p h c", h=HEADS),
                                  AX.X, ALU.add).then_inc(pre, 1)
            dve.wait_ge(pre, 7)
            for i in range(2):
                dve.tensor_scalar(w12[:, i, C:WX], w12[:, i, C:WX], SLOPE, None, ALU.mult).then_inc(w_ready, 1)
            for c in range(2, SM):
                compare(c)
            dve.wait_ge(passed_used, SM)
            for q, bank in enumerate(quarters):
                dve.tensor_copy(edge_tile_row[:, q * QW:(q + 1) * QW], bank[0:1, 0:QW]).then_inc(tiles_row, 1)
            dve.wait_ge(tiles_row, 4)
            dve.tensor_tensor(node_tile_row[:, 0:NS], iota[0:1, :], edge_tile_row, ALU.subtract).then_inc(pre, 1)
            dve.memset(node_tile_row[:, NS:NS + K], 0).then_inc(node_tiles_ready, 1)
            dve.wait_ge(col_ps, 1)
            dve.tensor_copy(edge_tile_col[:, :], psT[:, 0:SM]).then_inc(col_ready, 1)
            dve.tensor_tensor(first_node[:, :], step_no[:, :], psT[:, 0:SM], ALU.subtract).then_inc(pre, 1)
            dve.wait_ge(pre, 9)
            dve.tensor_scalar(first_node[:, :], first_node[:, :], float(P), None, ALU.mult).then_inc(pre, 1)
            dve.tensor_scalar(node_tile_row[:, 0:NS], node_tile_row[:, 0:NS], float(NT), None, ALU.min).then_inc(node_tiles_ready, 1)
            dve.memset(hj[:, NT:NA, :], 0.0).then_inc(fills, 1)
            dve.memset(src_idx[:, NS:NS + 3 * K], 0).then_inc(fills, 1)
            dve.memset(neg_local[:, NS:NS + K], 0.0).then_inc(fills, 1)
            dve.memset(through[:, :, :, :, :], -BIG).then_inc(fills, 1)
            dve.wait_ge(pre, 10)
            def spread_table(m):
                if m >= 2:
                    dve.wait_ge(tab_ps, m - 1)
                dve.wait_ge(table_in[m % TR], 16 * (m // TR + 1))
                dve.tensor_copy(tab_f[:, m % 2, 0, :], tables[:, m % TR, 0, :]).then_inc(tab_ready, 1)
                dve.tensor_scalar(local_s[:, m, :], tables[:, m % TR, 1, :], first_node[:, m:m + 1], None,
                                  ALU.subtract).then_inc(tab_ready, 1)

            def next_idx(G, ready):
                dve.tensor_copy(idx_g[:, slot(G) // K, :], src_idx[:, ds(number(G) * K, K)]).then_inc(ready, 1)

            spread_table(0)
            for m in range(SM):
                if m + 1 < SM:
                    spread_table(m + 1)
                bank = (psT, psC)[m % 2]
                at = slice(m * P, m * P + P)
                dve.wait_ge(tab_ps, m + 1)
                dve.tensor_copy(src_idx[:, at], bank[:, 0:P])
                dve.tensor_copy(weight[:, at], bank[:, 2 * P:3 * P]).then_inc(tab_out, 1)
                dve.tensor_scalar(neg_local[:, at], bank[:, P:2 * P], -1.0, None, ALU.mult).then_inc(local_out, 1)
                if m == 0:
                    dve.wait_ge(tab_out, 1)
                    dve.wait_ge(fills, 10)
                    for g in range(3):
                        next_idx((0, g), idx_ready)

            def next_local(G):
                dve.tensor_copy(neg_local_g[:, parity(G), :], neg_local[:, ds(number(G) * K, K)]).then_inc(neg_ready, 1)

            dve.wait_ge(local_out, SM)
            next_local((0, 0))
            dve.wait_ge(prev_in, 16)
            dve.tensor_tensor(prev_s, local_s, prev_s, ALU.not_equal).then_inc(pre, 1)
            dve.wait_ge(pre, 11)
            dve.tensor_scalar(prev_s, prev_s, -BIG, None, ALU.mult).then_inc(starts_made, 1)
            dve.wait_ge(starts_made, 1)
            dve.tensor_reduce(first_node[:, :], prev_s[:, :, 1:P], AX.X, ALU.min).then_inc(pre, 1)
            dve.wait_ge(pre, 12)
            dve.tensor_tensor(small[:, 1, :], first_node[:, :], prev_s[:, :, 0], ALU.add).then_inc(through_made, 1)
            dve.wait_ge(next_in, 16)
            dve.tensor_tensor(small[:, 2, :], first_node[:, :], small[:, 0, :], ALU.add).then_inc(through_made, 1)

            def relu(G, j):
                b = number(G) * J + j
                if not (early(G, 1) and j == 0):
                    dve.wait_ge(reduced, b)
                dve.wait_ge(U_ready, b + 1)
                dve.scalar_tensor_tensor(out=weighted[:, :].rearrange("p (k c) -> p k c", k=B),
                                         in0=psU[j % 2][:, :, 0:C], scalar=0.0,
                                         in1=a_relu[:, :].rearrange("p (o c) -> p o c", o=1).to_broadcast([P, B, C]),
                                         op0=ALU.max, op1=ALU.mult).then_inc(relu_done, 1)

            def reduce(G, j):
                dve.wait_ge(relu_done, number(G) * J + (j + 1))
                dve.tensor_reduce(logits[:, slot(G) // K, :, j * B:j * B + B].rearrange("p h k -> p k h"),
                                  weighted[:, :].rearrange("p (k h c) -> p k h c", k=B, h=HEADS), AX.X, ALU.add) \
                    .then_inc(reduced, 1)

            def add_linear(G, j):
                b = number(G) * J + j
                dve.wait_ge(reduced, b + 1)
                at = logits[:, slot(G) // K, :, j * B:j * B + B].rearrange("p h k -> p k h")
                dve.tensor_tensor(at, at, psU[j % 2][:, :, C:WX], ALU.add) \
                    .then_inc(logits_ready, 1)

            def flat(t, back=False):
                t = t.rearrange("o h s -> o (h s)")
                return t[:, ::-1] if back else t

            def scan_tiles(Q, back):
                q = number(Q)
                if not back:
                    dve.wait_ge(flags_in[parity(Q)], (half(Q) + 1) * (16 * (2 * HEADS + 2)))
                    dve.wait_ge(logitsT, q + 1)
                    dve.tensor_tensor_scan(scan_a[:, :], starts[:, parity(Q), 0:P], psC[:, C_LOGITS:C_LOGITS + P], -BIG, ALU.add, ALU.max).then_inc(scan1, 1)
                else:
                    dve.wait_ge(scan1, q + 1)
                    dve.tensor_tensor_scan(scan_b[:, ::-1], starts[:, parity(Q), 1:P + 1][:, ::-1], scan_a[:, ::-1], -BIG,
                                           ALU.add, ALU.max).then_inc(scan2, 1)

            def carry(Q):
                dve.tensor_copy(last_max[:, :, 0:1], up[:, :, K:SLOTS]).then_inc(carry_sb, 1)

            def scan_group(Q):
                dve.wait_ge(carry_sb, number(Q) + 1)
                dve.wait_ge(ends_sb, number(Q) * 2 + 2)
                dve.tensor_tensor_scan(flat(up[:, :, :]), flat(through[0:1, parity(Q), 0]), flat(last_max[:, :, :]), -BIG,
                                       ALU.add, ALU.max).then_inc(scan_up, 1)
                dve.tensor_tensor_scan(flat(down[:, :, :], True), flat(through[0:1, parity(Q), 1], True), flat(first_max[:, :, :], True),
                                       -BIG, ALU.add, ALU.max).then_inc(scan_up, 1)

            def scan_again(Q, back):
                q = number(Q)
                if not back:
                    dve.wait_ge(updown_ps, q + 1)
                    dve.tensor_tensor_scan(scan_a[:, :], starts[:, parity(Q), 0:P], psC[:, C_LOGITS:C_LOGITS + P], psC[:, C_UPDOWN:C_UPDOWN + 1], ALU.add, ALU.max).then_inc(scan3, 1)
                else:
                    dve.wait_ge(scan3, q + 1)
                    dve.tensor_tensor_scan(scan_b[:, ::-1], starts[:, parity(Q), 1:P + 1][:, ::-1], scan_a[:, ::-1], psC[:, C_UPDOWN + 1:C_UPDOWN + 2],
                                           ALU.add, ALU.max).then_inc(scan4, 1)

            def subtract_max(Q):
                q = number(Q)
                dve.wait_ge(maxT, q + 1)
                dve.tensor_tensor(shift[:, 0, :], last_max[:, :, 0], psC[0:1, C_MAX:C_MAX + P].rearrange("o (h k) -> o h k", k=K)[:, :, 0],
                                  ALU.subtract).then_inc(shift1, 1)
                if not early(Q, 1):
                    dve.wait_ge(weights_ready, q)
                dve.tensor_tensor(below[:, :], logits[:, slot(Q) // K, :, :].rearrange("p h k -> p (h k)"), psC[:, C_MAX:C_MAX + P],
                                  ALU.subtract).then_inc(below_ready, 1)
                dve.wait_ge(shift1, q + 1)
                dve.tensor_scalar(shift[:, 1, :], shift[:, 0, :], 0.0, None, ALU.min).then_inc(shift2, 1)

            def copy_shift(Q):
                dve.wait_ge(rescale_ps, number(Q) + 1)
                dve.tensor_copy(rescale[:, parity(Q), :], psC[:, C_SHIFT:C_SHIFT + HEADS]).then_inc(rescale_log, 1)

            tile_of = [0] * K

            def node_tiles(G):
                _, values = nc.values_load_multi_w_load_instructions(
                    node_tile_row[0:1, ds(number(G) * K, K)], [mybir.EngineType.DVE], min_val=0, max_val=NA - 1,
                    skip_runtime_bounds_check_because="a step's node tile is at most NT")
                tile_of[:] = values

            def scale_first(Q):
                q = number(Q)
                dve.wait_ge(rescale_sb, q + 1)
                if not early(Q, 1):
                    dve.wait_ge(added, q * K)
                tile = ds(tile_of[0], 1)
                num = acc[:, tile, :, 0:C].rearrange("p o e (h c) -> p (o e) h c", h=HEADS)
                den = acc[:, tile, :, C:WX].rearrange("p o e h -> p (o e) h")
                dve.tensor_tensor(num, num, rescale[:, parity(Q), :].rearrange("p (e h o) -> p e h o", e=1, o=1).to_broadcast([P, 2, HEADS, CH]),
                                  ALU.mult).then_inc(rescaled, 1)
                dve.tensor_tensor(den, den, rescale[:, parity(Q), :].rearrange("p (e h) -> p e h", e=1).to_broadcast([P, 2, HEADS]),
                                  ALU.mult).then_inc(rescaled, 1)

            def messages(Q, j):
                if j == 0:
                    dve.wait_ge(weights_ready, number(Q) + 1)
                s0 = slot(Q) + j * B
                hi = rows[:, s0:s0 + B, 0:C].rearrange("p k (h c) -> p k h c", h=HEADS)
                dve.tensor_tensor(hi, hi, rows[:, s0:s0 + B, C:WX].rearrange("p k (h o) -> p k h o", o=1).to_broadcast([P, B, HEADS, CH]),
                                  ALU.mult).then_inc(msg_ready, 1)

            def add(Q, k, width, summed, done):
                q = number(Q)
                if k % 2 == 0:
                    dve.wait_ge(summed, q * (K // 2) + (k // 2 + 1))
                if not (early(Q, 1) and k < 2):
                    dve.wait_ge(done, q * K + (k - 1))
                at = acc[:, ds(tile_of[k], 1), k % 2, 0:width].rearrange("p o w -> p (o w)")
                dve.tensor_tensor(at, at, psP[k // 2 % 2][:, k % 2 * 256:k % 2 * 256 + width], ALU.add).then_inc(done, 1)

            def weave(G, spreads=True, chain=True, middle=True, summing=True):
                Q, O, L = (near(G, n) for n in (-1, -2, -3))

                def adds(j, i):
                    if summing:
                        add(L, j * B + 2 * i, WX, sums_ps, added)
                        add(L, j * B + 2 * i + 1, WX, sums_ps, added)

                if summing:
                    messages(L, 3)
                    node_tiles(L)
                    scale_first(L)
                if spreads:
                    next_idx(near(G, 3), idx_ready)
                    next_local(near(G, 1))
                if summing:
                    dve.wait_ge(rescaled, number(L) * 2 + 2)
                adds(0, 0)
                adds(0, 1)
                if spreads:
                    relu(G, 0)
                if middle:
                    subtract_max(O)
                if chain:
                    scan_tiles(Q, False)
                if spreads:
                    reduce(G, 0)
                if chain:
                    scan_tiles(Q, True)
                adds(1, 0)
                if spreads:
                    add_linear(G, 0)
                if chain:
                    carry(Q)
                adds(1, 1)
                if spreads:
                    relu(G, 1)
                if middle:
                    messages(O, 0)
                if chain:
                    scan_group(Q)
                adds(2, 0)
                if spreads:
                    reduce(G, 1)
                adds(2, 1)
                if spreads:
                    add_linear(G, 1)
                    relu(G, 2)
                if middle:
                    messages(O, 1)
                adds(3, 0)
                if spreads:
                    reduce(G, 2)
                adds(3, 1)
                if spreads:
                    add_linear(G, 2)
                if chain:
                    scan_again(Q, False)
                if spreads:
                    relu(G, 3)
                if chain:
                    scan_again(Q, True)
                if middle:
                    copy_shift(O)
                    messages(O, 2)
                if spreads:
                    reduce(G, 3)
                    add_linear(G, 3)

            dve.wait_ge(fills2, 1)
            groups(dve, lambda G: weave(G, chain=not early(G, 1), middle=not early(G, 2), summing=not early(G, 3)))
            weave(last_group(1), spreads=False)
            weave(last_group(2), spreads=False, chain=False)
            weave(last_group(3), spreads=False, chain=False, middle=False)

            def scales(rnd):
                v = fin_small[rnd]
                if rnd == 0:
                    den = acc[:, 0:NT, :, C:WX]
                    dve.tensor_tensor(den[:, :, 0, :], den[:, :, 0, :], den[:, :, 1, :], ALU.add).then_inc(v, 1)
                    dve.wait_ge(v, 1)
                    dve.tensor_scalar(den[:, :, 0, :], den[:, :, 0, :], 1e-30, None, ALU.max).then_inc(v, 1)
                    dve.wait_ge(v, 2)
                    dve.reciprocal(den[:, :, 0, :], den[:, :, 0, :]).then_inc(v, 1)
                    dve.wait_ge(v, 3)
                else:
                    count, top, part, inverse, keep, share = (fin[:, i, :] for i in range(6))
                    dve.tensor_tensor(count, acc[:, 0:NT, 0, C], acc[:, 0:NT, 1, C], ALU.add).then_inc(v, 1)
                    dve.wait_ge(v, 1)
                    dve.tensor_scalar(top, count, EPS_COUNT, None, ALU.max).then_inc(v, 1)
                    dve.tensor_scalar(part, count, EPS_COUNT, MIX, ALU.is_gt, ALU.mult).then_inc(v, 1)
                    dve.wait_ge(v, 3)
                    dve.reciprocal(inverse, top).then_inc(v, 1)
                    dve.tensor_scalar(keep, part, -1.0, 2.0, ALU.mult, ALU.add).then_inc(v, 1)
                    dve.wait_ge(v, 5)
                    dve.tensor_tensor(share, inverse, part, ALU.mult).then_inc(v, 1)
                    dve.wait_ge(v, 6)

            def scale_sums(rnd, c):
                dve.wait_ge(fin_merged[rnd], c + 1)
                if c >= 2:
                    dve.wait_ge(fin_x[rnd], c - 1)
                w, total = work[:, c % 2], acc[:, chunk(c), 0, 0:C]
                if rnd == 0:
                    dve.tensor_tensor(w.rearrange("p t (h c) -> p t h c", h=HEADS), total.rearrange("p t (h c) -> p t h c", h=HEADS),
                                      acc[:, chunk(c), 0, C:WX].rearrange("p t (h o) -> p t h o", o=1).to_broadcast([P, CT, HEADS, CH]),
                                      ALU.mult).then_inc(fin_w[rnd], 1)
                else:
                    dve.tensor_tensor(w, total, fin[:, 5, chunk(c)].rearrange("p (t o) -> p t o", o=1).to_broadcast([P, CT, C]),
                                      ALU.mult).then_inc(fin_w[rnd], 1)

            def final(rnd):
                scales(rnd)
                scale_sums(rnd, 0)
                for c in range(CHUNKS + 1):
                    if c + 1 < CHUNKS:
                        scale_sums(rnd, c + 1)
                    if c < CHUNKS:
                        if rnd == 1:
                            dve.wait_ge(fin_w[rnd], c + 1)
                            for i in range(CT):
                                xt = x_sb[:, c * CT + i, :]
                                op = dve.scalar_tensor_tensor(out=xt, in0=xt, scalar=fin[:, 4, c * CT + i:c * CT + i + 1],
                                                              in1=work[:, c % 2, i, :], op0=ALU.mult, op1=ALU.add)
                            op.then_inc(fin_x[rnd], 1)
                        dve.wait_ge(fin_x[rnd], c + 1)
                        if c >= 1:
                            dve.wait_ge(fin_var[rnd], c)
                        for i in range(CT):
                            op = dve.bn_stats(stats[:, i, :], x_sb[:, c * CT + i, :])
                        op.then_inc(fin_stats[rnd], 1)
                        dve.wait_ge(fin_stats[rnd], c + 1)
                        if c >= 2:
                            dve.wait_ge(fin_done[rnd], (c - 1) * CT)
                        for i in range(CT):
                            op = dve.bn_aggr(mv[:, c % 2, i, :], stats[:, i, :])
                        op.then_inc(fin_var[rnd], 1)
                    if c >= 1:
                        m, s = mv[:, (c - 1) % 2], rstd[:, (c - 1) % 2]
                        dve.wait_ge(fin_std[rnd], c)
                        dve.reciprocal(s[:, 1, :], s[:, 0, :]).then_inc(fin_inv[rnd], 1)
                        dve.wait_ge(fin_inv[rnd], c)
                        dve.scalar_tensor_tensor(out=s[:, 2, :], in0=m[:, :, 0], scalar=-1.0, in1=s[:, 1, :],
                                                 op0=ALU.mult, op1=ALU.mult).then_inc(fin_rs[rnd], 1)

            dve.wait_ge(added, NS)
            final(0)

            dve.memset(acc[:, :, 0, :], 0.0).then_inc(acc1_zero, 1)
            dve.memset(rows[:, :, C:C + 1], 1.0).then_inc(acc1_zero, 1)
            dve.wait_ge(acc1_zero, 2)
            dve.wait_ge(S_ready, NS // B + J)

            def onehot1(G, j):
                if not early(G, RING):
                    dve.wait_ge(sums1_ps, number(G) * (2 * J) + (2 * (j + 1) - 2 * RING * J))
                for k in range(j * B, j * B + B):
                    op = dve.tensor_scalar(S[:, slot(G) + k, :], neg_iota[:, :], neg_local_g[:, parity(G), k:k + 1],
                                           weight_g[:, parity(G), k:k + 1], ALU.is_equal, ALU.mult)
                op.then_inc(S1_ready, 1)

            def weave1(G):
                g = number(G)
                next_idx(near(G, 3), idx1_ready)
                dve.tensor_copy(neg_local_g[:, parity(G), :], neg_local[:, ds(g * K, K)]).then_inc(local1_ready, 1)
                dve.tensor_copy(weight_g[:, parity(G), :], weight[:, ds(g * K, K)]).then_inc(local1_ready, 1)
                node_tiles(G)
                dve.wait_ge(local1_ready, g * 2 + 2)
                for j in range(J):
                    onehot1(G, j)
                if early(G, 1):
                    dve.wait_ge(acc1_odd_zero, 1)
                for k in range(K):
                    add(G, k, W1, sums1_ps, added1)

            for g in range(3):
                next_idx((0, g), idx1_ready)
            groups(dve, weave1)
            dve.wait_ge(added1, NS)
            final(1)


_INS = ["x", "src", "dst", "edge_weight", "L0_gnn_w1", "L0_gnn_w2", "L0_gnn_a"]


def kernel(**inputs):
    import numpy as _np
    import concourse.bacc as _bacc
    from concourse import mybir as _mybir
    from concourse.bass_utils import run_bass_kernel_spmd as _run

    nc = _bacc.Bacc("TRN2", target_bir_lowering=False, num_devices=1)
    arrays, args = {}, []
    for name in _INS:
        v = _np.ascontiguousarray(inputs[name])
        arrays[f"in_{name}"] = v
        args.append(nc.dram_tensor(f"in_{name}", v.shape, _mybir.dt.from_np(v.dtype), kind="ExternalInput").ap())
    args.append(nc.dram_tensor("out_0", inputs["x"].shape, _mybir.dt.float32, kind="ExternalOutput").ap())
    graph_kernel(nc, *args)
    r = _run(nc, [arrays], core_ids=[0])
    return r.results[0]["out_0"]
```
